# Optimizing a Trainium2 kernel written in Bass

```python
import numpy as np
import jax
import jax.numpy as jnp

def _softmax(x, axis=-1):
    return jax.nn.softmax(x, axis=axis)

def _gelu(x):
    return jax.nn.gelu(x, approximate=True)

def _silu(x):
    return jax.nn.silu(x)

def _sigmoid(x):
    return jax.nn.sigmoid(x)

def _layernorm(x, axis=-1, eps=1e-05):
    m = jnp.mean(x, axis=axis, keepdims=True)
    v = jnp.var(x, axis=axis, keepdims=True)
    return (x - m) / jnp.sqrt(v + eps)

def _scatter_add(tgt, idx, src, axis=0):
    return tgt.at[idx].add(src)

def _segment_sum(src, seg, n):
    return jax.ops.segment_sum(src, seg, n)
kernel_name = 'mk_xattn_ffn_d1_seqx_r8_de2672'

def setup_inputs(seed: int=0):
    np.random.seed(seed)
    _w = jnp.asarray

    def _rec_inputs():
        import jax
        import jax.numpy as jnp
        _rk = jax.random.key(seed)
        x = 7.22e-05 + 1 * jax.random.normal(jax.random.fold_in(_rk, 1), (32, 64, 256), jnp.float32)
        _lenS = 64 - jax.random.randint(jax.random.fold_in(_rk, 7), (32,), 0, max(1, 64 // 4) + 1, jnp.int32)
        _lenS2 = 64 - jax.random.randint(jax.random.fold_in(_rk, 8), (32,), 0, max(1, 64 // 4) + 1, jnp.int32)
        _ctx_1024P = jax.random.normal(jax.random.fold_in(_rk, 11), (32, 16, 128), jnp.float32)
        _ctx_1024c = jax.random.dirichlet(jax.random.fold_in(_rk, 511), 0.3 * jnp.ones((16,), jnp.float32), (32, 64))
        _ctx_1024t = jnp.einsum('bsk,bkd->bsd', _ctx_1024c, _ctx_1024P)
        _ctx_1024t = _ctx_1024t * jax.lax.rsqrt(jnp.mean(jnp.square(_ctx_1024t)) + 1e-12) * 0.953939
        ctx_1024 = -1.39393e-06 + 0.999914 * (_ctx_1024t + 0.3 * jax.random.normal(jax.random.fold_in(_rk, 611), (32, 64, 128), jnp.float32))
        fside_BxSx2_0 = jax.random.uniform(jax.random.fold_in(_rk, 12), (32, 64, 2), jnp.float32, 0.0, 0.999707)
        return (x, ctx_1024, fside_BxSx2_0)
    x, ctx_1024, fside_BxSx2_0 = _rec_inputs()

    def _L0_xattn_setup():
        import jax, jax.numpy as jnp
        import numpy as np
        DIM = 256
        CTX_DIM = 128
        N_HEADS = 32
        HEAD_DIM = DIM // N_HEADS
        POS_DIM = 2
        B, N, CTXN = (2, 256, 256)
        ROPE_BASE = 10000.0

        def apply_axial_rope(x, pos):
            b, n, h, d = x.shape
            p = pos.shape[-1]
            dpa = d // p
            half = dpa // 2
            freqs = ROPE_BASE ** (-jnp.arange(half, dtype=x.dtype) / half)
            ang = pos[..., :, None] * freqs
            cos = jnp.cos(ang)[:, :, None, :, :]
            sin = jnp.sin(ang)[:, :, None, :, :]
            xr = x.reshape(b, n, h, p, half, 2)
            x1, x2 = (xr[..., 0], xr[..., 1])
            out = jnp.stack([x1 * cos - x2 * sin, x1 * sin + x2 * cos], axis=-1)
            return out.reshape(b, n, h, d)
        key = jax.random.key(seed)
        ks = jax.random.split(key, 8)
        x = jax.random.normal(ks[0], (B, N, DIM), jnp.float32)
        ctx = jax.random.normal(ks[1], (B, CTXN, CTX_DIM), jnp.float32)
        pos_map = jax.random.uniform(ks[2], (B, N, POS_DIM), jnp.float32)
        ctx_pos_map = jax.random.uniform(ks[3], (B, CTXN, POS_DIM), jnp.float32)
        Wq = jax.random.normal(ks[4], (DIM, DIM), jnp.float32) / np.sqrt(DIM)
        Wkv = jax.random.normal(ks[5], (CTX_DIM, 2 * DIM), jnp.float32) / np.sqrt(CTX_DIM)
        Wout = jax.random.normal(ks[6], (DIM, DIM), jnp.float32) / np.sqrt(DIM)
        bout = jnp.zeros((DIM,), jnp.float32)
        return {'x': x, 'ctx': ctx, 'pos_map': pos_map, 'ctx_pos_map': ctx_pos_map, 'Wq': Wq, 'Wkv': Wkv, 'Wout': Wout, 'bout': bout}
    _L0_xattn_all = _L0_xattn_setup()
    _L0_xattn_in = {k: v for k, v in _L0_xattn_all.items() if k in ('Wq', 'Wkv', 'Wout', 'bout')}
    del _L0_xattn_all

    def _L0_ffn_setup():
        import jax, jax.numpy as jnp
        import numpy as np
        LN_EPS = 1e-05
        L2_EPS = 1e-12

        def _l2norm(v, axis):
            n = jnp.sqrt(jnp.sum(v * v, axis=axis, keepdims=True))
            return v / jnp.maximum(n, L2_EPS)
        key = jax.random.key(seed)
        ks = jax.random.split(key, 4)
        B, N, D, E, S, H = (8, 256, 256, 16, 128, 64)
        x = jax.random.normal(ks[0], (B, N, D), dtype=jnp.float32)
        mu = jax.random.normal(ks[1], (D, E, S), dtype=jnp.float32) / np.sqrt(D)
        W1 = jax.random.normal(ks[2], (E, D, H), dtype=jnp.float32) * np.sqrt(2.0 / D)
        W2 = jax.random.normal(ks[3], (E, H, D), dtype=jnp.float32) * np.sqrt(2.0 / (H + D))
        return {'x': x, 'gamma': jnp.ones((D,), jnp.float32), 'beta': jnp.zeros((D,), jnp.float32), 'mu': mu, 'scale': jnp.ones((1,), jnp.float32), 'W1': W1, 'b1': jnp.zeros((E, H), jnp.float32), 'W2': W2, 'b2': jnp.zeros((E, D), jnp.float32)}
    _L0_ffn_all = _L0_ffn_setup()
    _L0_ffn_in = {k: v for k, v in _L0_ffn_all.items() if k in ('gamma', 'beta', 'mu', 'scale', 'W1', 'b1', 'W2', 'b2')}
    del _L0_ffn_all
    return {'x': x, 'ctx_1024': ctx_1024, 'fside_BxSx2_0': fside_BxSx2_0, 'L0_xattn_Wq': _L0_xattn_in['Wq'], 'L0_xattn_Wkv': _L0_xattn_in['Wkv'], 'L0_xattn_Wout': _L0_xattn_in['Wout'], 'L0_xattn_bout': _L0_xattn_in['bout'], 'L0_ffn_gamma': _L0_ffn_in['gamma'], 'L0_ffn_beta': _L0_ffn_in['beta'], 'L0_ffn_mu': _L0_ffn_in['mu'], 'L0_ffn_scale': _L0_ffn_in['scale'], 'L0_ffn_W1': _L0_ffn_in['W1'], 'L0_ffn_b1': _L0_ffn_in['b1'], 'L0_ffn_W2': _L0_ffn_in['W2'], 'L0_ffn_b2': _L0_ffn_in['b2']}

def reference(x, ctx_1024, fside_BxSx2_0, L0_xattn_Wq, L0_xattn_Wkv, L0_xattn_Wout, L0_xattn_bout, L0_ffn_gamma, L0_ffn_beta, L0_ffn_mu, L0_ffn_scale, L0_ffn_W1, L0_ffn_b1, L0_ffn_W2, L0_ffn_b2):
    import jax
    import jax.numpy as jnp

    def _L0_xattn_ref(x, ctx, pos_map, ctx_pos_map, Wq, Wkv, Wout, bout):
        import jax, jax.numpy as jnp
        import numpy as np
        DIM = 256
        CTX_DIM = 128
        N_HEADS = 32
        HEAD_DIM = DIM // N_HEADS
        POS_DIM = 2
        B, N, CTXN = (2, 256, 256)
        ROPE_BASE = 10000.0

        def apply_axial_rope(x, pos):
            b, n, h, d = x.shape
            p = pos.shape[-1]
            dpa = d // p
            half = dpa // 2
            freqs = ROPE_BASE ** (-jnp.arange(half, dtype=x.dtype) / half)
            ang = pos[..., :, None] * freqs
            cos = jnp.cos(ang)[:, :, None, :, :]
            sin = jnp.sin(ang)[:, :, None, :, :]
            xr = x.reshape(b, n, h, p, half, 2)
            x1, x2 = (xr[..., 0], xr[..., 1])
            out = jnp.stack([x1 * cos - x2 * sin, x1 * sin + x2 * cos], axis=-1)
            return out.reshape(b, n, h, d)
        b, n, _ = x.shape
        ctx_n = ctx.shape[1]
        q = (x @ Wq).reshape(b, n, N_HEADS, HEAD_DIM)
        k, v = jnp.split(ctx @ Wkv, 2, axis=-1)
        k = k.reshape(b, ctx_n, N_HEADS, HEAD_DIM)
        v = v.reshape(b, ctx_n, N_HEADS, HEAD_DIM)
        q = apply_axial_rope(q, pos_map)
        k = apply_axial_rope(k, ctx_pos_map)
        scale = 1.0 / np.sqrt(HEAD_DIM).astype(np.float32)
        logits = jnp.einsum('bqhd,bkhd->bhqk', q, k) * scale
        w = jax.nn.softmax(logits, axis=-1)
        attn = jnp.einsum('bhqk,bkhd->bqhd', w, v)
        attn = attn.reshape(b, n, N_HEADS * HEAD_DIM)
        return attn @ Wout + bout

    def _L0_ffn_ref(x, gamma, beta, mu, scale, W1, b1, W2, b2):
        import jax, jax.numpy as jnp
        import numpy as np
        LN_EPS = 1e-05
        L2_EPS = 1e-12

        def _l2norm(v, axis):
            n = jnp.sqrt(jnp.sum(v * v, axis=axis, keepdims=True))
            return v / jnp.maximum(n, L2_EPS)
        B, N, D = x.shape
        _, E, S = mu.shape
        mean = jnp.mean(x, axis=-1, keepdims=True)
        var = jnp.mean(jnp.square(x - mean), axis=-1, keepdims=True)
        x_ln = (x - mean) / jnp.sqrt(var + LN_EPS) * gamma + beta
        x_n = _l2norm(x_ln, -1) * scale
        mu_n = _l2norm(mu, 0)
        logits = jnp.einsum('bnd,des->bnes', x_n, mu_n)
        dispatch = jax.nn.softmax(logits, axis=1)
        combine = jax.nn.softmax(logits.reshape(B, N, E * S), axis=-1)
        slot_in = jnp.einsum('bnd,bnes->besd', x_ln, dispatch)
        h = jax.nn.gelu(jnp.einsum('besd,edh->besh', slot_in, W1) + b1[None, :, None, :], approximate=False)
        slot_out = jnp.einsum('besh,ehd->besd', h, W2) + b2[None, :, None, :]
        out = jnp.einsum('bsd,bns->bnd', slot_out.reshape(B, E * S, D), combine)
        return out
    x = x + _L0_xattn_ref(_layernorm(x, axis=-1), ctx_1024, fside_BxSx2_0, fside_BxSx2_0, L0_xattn_Wq, L0_xattn_Wkv, L0_xattn_Wout, L0_xattn_bout)
    x = x + _L0_ffn_ref(_layernorm(x, axis=-1), L0_ffn_gamma, L0_ffn_beta, L0_ffn_mu, L0_ffn_scale, L0_ffn_W1, L0_ffn_b1, L0_ffn_W2, L0_ffn_b2)
    return x

_drawn_inputs = setup_inputs


def setup_inputs(seed=0):
    import zlib

    import numpy as np

    out = dict(_drawn_inputs(seed))
    spreads = {'L0_xattn_bout': (0.0, 0.1),
     'L0_ffn_gamma': (1.0, 0.6),
     'L0_ffn_beta': (0.0, 0.675),
     'L0_ffn_b1': (0.0, 0.8),
     'L0_ffn_b2': (0.0, 0.367)}
    factors = {'L0_ffn_mu': 8.0}
    for name, (base, spread) in spreads.items():
        noise = np.random.default_rng([zlib.crc32(name.encode()), seed]).standard_normal(out[name].shape)
        drawn = base * np.exp(spread * noise) if base else spread * noise
        out[name] = jnp.asarray(drawn.astype(out[name].dtype))
    for name, factor in factors.items():
        out[name] = (out[name] * factor).astype(out[name].dtype)
    return out
```

```python
import concourse.bass as bass
from concourse import mybir
from contextlib import ExitStack

F32 = mybir.dt.float32
ALU = mybir.AluOpType
ACT = mybir.ActivationFunctionType
AX = mybir.AxisListType

P = 128
BATCH, SEQ, DIM, CDIM = 32, 64, 256, 128
TILES = BATCH * SEQ // P
KD = DIM // P
HEADS, HD = 32, 8
EXPERTS, SLOTS, HID = 16, 128, 64
ES = EXPERTS * SLOTS
BANK = 512
LN_EPS = 1e-5
L2_EPS = 1e-12
ROPE_FREQ = (1.0, 0.01)
SAFE = 80.0
GROUPS = 4
HC = HID + 1


def wait(eng, sem, value):
    if isinstance(value, int) and value <= 0:
        return
    eng.wait_ge(sem, value)


def build(nc, x, ctx_in, pos, Wq, Wkv, Wout, bout, gamma, beta, mu, scale, W1, b1, W2, b2, out):
    ctx = ExitStack()
    with ctx:
        def sb(name, *shape):
            return ctx.enter_context(nc.sbuf_tensor(name, list(shape), F32))

        def sem(name):
            return ctx.enter_context(nc.semaphore(name))

        ident = sb("ident", P, P)
        ones = sb("ones", P, P)
        wq = sb("wq", P, KD, DIM)
        wkv = sb("wkv", P, 2 * DIM)
        wo = sb("wo", P, KD, DIM)
        mun = sb("mun", P, KD, ES)
        w1 = sb("w1", P, KD, EXPERTS * HID)
        w2 = sb("w2", P, EXPERTS // 2, DIM)
        b1b = sb("b1b", P, EXPERTS, HID)
        b2s = sb("b2s", EXPERTS, DIM)
        boutb = sb("boutb", P, DIM)
        gammab = sb("gammab", P, DIM)
        betab = sb("betab", P, DIM)
        scaleb = sb("scaleb", P, 1)
        nshift = sb("nshift", P, 1)
        posb = sb("posb", P, TILES, 2)
        ang = sb("ang", P, 2, TILES, 2, 2)
        turns = sb("turns", P, 2, TILES, 2, 2)
        cosb = sb("cosb", P, TILES, 8)
        sinb = sb("sinb", P, TILES, 8)
        mhalf = sb("mhalf", P, TILES)
        threehalf = sb("threehalf", P, TILES)
        hone = sb("hone", P, 2, 32)

        xa = sb("xa", P, TILES, DIM)
        ctile = sb("ctile", P, 2, CDIM)
        st1 = sb("st1", P, TILES, 6)
        ln1 = sb("ln1", P, 8, TILES)
        xc = sb("xc", P, 2, DIM)
        xn = sb("xn", P, 2, DIM)
        xT = sb("xT", P, 3, P)
        ra = sb("ra", P, 64, 8)
        rb = sb("rb", P, 64, 8)
        qr = sb("qr", P, DIM)
        kz = sb("kz", P, 2, 544)
        qT = sb("qT", P, 2, P)
        kT = sb("kT", P, 2, 4, P)
        vb = sb("vb", P, 2, 2, 2, 272)
        mx = sb("mx", P, GROUPS, 8)
        pb = sb("pb", P, 2, GROUPS, 8, SEQ)
        pT = sb("pT", P, 16, P)
        rc = sb("rc", P, DIM)
        oT = sb("oT", P, DIM)
        st2 = sb("st2", P, TILES, 6)
        ln2 = sb("ln2", P, 8, TILES)
        xl = sb("xl", P, 2, DIM)
        sq = sb("sq", P, DIM)
        ss = sb("ss", P, 2)
        sm2 = sb("sm2", P, 2, 8)
        rn = sb("rn", P, 2)
        xlT = sb("xlT", P, KD, P)
        eb = sb("eb", P, EXPERTS, SLOTS)
        es = sb("es", P, EXPERTS)
        rs = sb("rs", P, 2)
        eT = sb("eT", P, EXPERTS, P)
        xw = sb("xw", P, EXPERTS, 2 * HC)
        rh = sb("rh", P, EXPERTS, 2)
        hb = sb("hb", P, EXPERTS, 2, HID)
        gT = sb("gT", P, EXPERTS // 2, P)
        esT = sb("esT", EXPERTS, P)
        yo = sb("yo", P, 2, DIM)

        bank = [ctx.enter_context(nc.psum_tensor(f"bank{i}", [P, BANK], F32)) for i in range(8)]

        x_loaded = [sem("x_loaded0"), sem("x_loaded1")]
        wa_loaded = sem("wa_loaded")
        pos_loaded = sem("pos_loaded")
        mu_loaded = sem("mu_loaded")
        wb_loaded = sem("wb_loaded")
        ctx_loaded = [sem("ctx_loaded0"), sem("ctx_loaded1")]
        ident_step = sem("ident_step")
        consts_pool = sem("consts_pool")
        consts_dve = sem("consts_dve")
        ang_step = sem("ang_step")
        ang_ready = sem("ang_ready")
        sin_ready = sem("sin_ready")
        rope_ready = sem("rope_ready")
        musq_ready = sem("musq_ready")
        muss_ready = sem("muss_ready")
        munorm_ready = sem("munorm_ready")
        mu_step = sem("mu_step")
        mu_ready = sem("mu_ready")
        shift_step = sem("shift_step")
        shift_ready = sem("shift_ready")
        st1_ready = sem("st1_ready")
        var1_step = sem("var1_step")
        var1_ready = sem("var1_ready")
        r1_step = sem("r1_step")
        r1_ready = sem("r1_ready")
        xc_done = sem("xc_done")
        xn_ready = sem("xn_ready")
        xb_ready = sem("xb_ready")
        xT_filled = sem("xT_filled")
        xT_ready = sem("xT_ready")
        qk_filled = sem("qk_filled")
        v_filled = sem("v_filled")
        ropeab_done = sem("ropeab_done")
        qk_roped = sem("qk_roped")
        v_ready = sem("v_ready")
        kq_filled = sem("kq_filled")
        kq_ready = sem("kq_ready")
        s_filled = sem("s_filled")
        max_done = sem("max_done")
        sub_done = sem("sub_done")
        p_ready = sem("p_ready")
        pT_filled = sem("pT_filled")
        pT_act = sem("pT_act")
        pT_dve = sem("pT_dve")
        o_filled = sem("o_filled")
        rc_done = sem("rc_done")
        oT_ready = sem("oT_ready")
        a_filled = sem("a_filled")
        x1_ready = sem("x1_ready")
        st2_ready = sem("st2_ready")
        var_step = sem("var_step")
        var_ready = sem("var_ready")
        r2_step = sem("r2_step")
        r2_ready = sem("r2_ready")
        z_ready = sem("z_ready")
        aff_step = sem("aff_step")
        xl_ready = sem("xl_ready")
        ss_ready = sem("ss_ready")
        ss_clamped = sem("ss_clamped")
        rn_step = sem("rn_step")
        rn_ready = sem("rn_ready")
        xlT_filled = sem("xlT_filled")
        xlT_ready = sem("xlT_ready")
        l_filled = sem("l_filled")
        e_ready = sem("e_ready")
        xw_filled = sem("xw_filled")
        xw_ready = sem("xw_ready")
        eT_filled = sem("eT_filled")
        eT_act = sem("eT_act")
        eT_dve = sem("eT_dve")
        es_ready = sem("es_ready")
        h_filled = sem("h_filled")
        rh_done = sem("rh_done")
        hn_ready = sem("hn_ready")
        h_ready = sem("h_ready")
        g_filled = sem("g_filled")
        gT_act = sem("gT_act")
        gT_dve = sem("gT_dve")
        esT_filled = sem("esT_filled")
        esT_ready = sem("esT_ready")
        rs_step = sem("rs_step")
        y_filled = sem("y_filled")
        yo_ready = sem("yo_ready")
        stored = [sem("stored0"), sem("stored1")]

        x_d = x.rearrange("b s d -> (b s) d").rearrange("(t p) d -> p t d", p=P)
        ctx_d = ctx_in.rearrange("b s d -> (b s) d").rearrange("(t p) d -> p t d", p=P)
        pos_d = pos.rearrange("b s c -> (b s) c").rearrange("(t p) c -> p t c", p=P)
        out_d = out.rearrange("b s d -> (b s) d").rearrange("(t p) d -> p t d", p=P)

        def row(v, n):
            return v.rearrange("(a d) -> a d", a=1).broadcast_to([P, n])

        PER = BANK // (2 * HC)
        HG = [range(i, min(i + PER, EXPERTS)) for i in range(0, EXPERTS, PER)]
        GG = [(HG[i][0], HG[min(i + 1, len(HG) - 1)][-1] + 1) for i in range(0, len(HG), 2)]
        W_A = 5 * 16
        W_B = 7 * 16

        block = ctx.enter_context(nc.Block())

        @block.sync
        def _(sp):
            def load_ctx(t, p):
                wait(sp, xT_filled, t - 1)
                sp.dma_start(ctile[:, p, :], ctx_d[:, t, :]).then_inc(ctx_loaded[p], 16)

            def store(t, p):
                sp.wait_ge(yo_ready, t + 1)
                sp.dma_start(out_d[:, t, :], yo[:, p, :]).then_inc(stored[p], 16)

            sp.dma_start(xa[:, 0:2, :], x_d[:, 0:2, :]).then_inc(x_loaded[0], 16)
            load_ctx(0, 0)
            sp.dma_start(wq[:], Wq.rearrange("(k p) n -> p k n", p=P)).then_inc(wa_loaded, 16)
            sp.dma_start(wkv[:], Wkv).then_inc(wa_loaded, 16)
            sp.dma_start(boutb[:], row(bout, DIM)).then_inc(wa_loaded, 16)
            sp.dma_start(scaleb[:], row(scale, 1)).then_inc(wa_loaded, 16)
            sp.dma_start(posb[:], pos_d).then_inc(pos_loaded, 16)
            load_ctx(1, 1)
            sp.dma_start(xa[:, 2:TILES, :], x_d[:, 2:TILES, :]).then_inc(x_loaded[1], 16)
            sp.dma_start(mun[:], mu.rearrange("(k p) e s -> p k (e s)", p=P)).then_inc(mu_loaded, 16)
            sp.dma_start(wo[:], Wout.rearrange("(k p) n -> p k n", p=P)).then_inc(wa_loaded, 16)
            for k in range(KD):
                sp.dma_start(w1[:, k, :].rearrange("p (e h) -> p e h", h=HID),
                             W1[:, k * P:(k + 1) * P, :].rearrange("e p h -> p e h")).then_inc(wb_loaded, 16)
            sp.dma_start(w2[:], W2.rearrange("e h d -> (e h) d").rearrange("(k p) d -> p k d", p=P))\
                .then_inc(wb_loaded, 16)
            sp.dma_start(b1b[:].rearrange("p e h -> p (e h)"), row(b1.rearrange("e h -> (e h)"), EXPERTS * HID))\
                .then_inc(wb_loaded, 16)
            sp.dma_start(b2s[:], b2).then_inc(wb_loaded, 16)
            sp.dma_start(gammab[:], row(gamma, DIM)).then_inc(wb_loaded, 16)
            sp.dma_start(betab[:], row(beta, DIM)).then_inc(wb_loaded, 16)
            with sp.Fori(1, TILES // 2) as i:
                for p in range(2):
                    load_ctx(i * 2 + p, p)
            with sp.Fori(0, TILES // 2) as i:
                for p in range(2):
                    store(i * 2 + p, p)
            for p in range(2):
                sp.wait_ge(stored[p], 16 * TILES // 2)

        @block.gpsimd
        def _(pool):
            g = nc.gpsimd
            g.memset(ident[:], 0.0).then_inc(ident_step, 1)
            pool.wait_ge(ident_step, 1)
            g.affine_select(out=ident[:], in_=ident[:], compare_op=ALU.not_equal, fill=1.0, base=0,
                            pattern=[[-1, P]], channel_multiplier=1).then_inc(consts_pool, 1)
            g.memset(mhalf[:], -0.5).then_inc(consts_pool, 1)
            g.memset(ones[:], 1.0).then_inc(consts_pool, 1)
            g.memset(threehalf[:], 1.5).then_inc(consts_pool, 1)
            pool.wait_ge(consts_pool, 4)

            def rsqrt(a, r, tmp, step, base):
                n = r.shape[1]
                g.tensor_tensor(tmp[0], a, mhalf[:, 0:n], ALU.pow).then_inc(step, 1)
                g.tensor_tensor(tmp[2], a, mhalf[:, 0:n], ALU.mult).then_inc(step, 1)
                pool.wait_ge(step, base + 1)
                g.tensor_tensor(tmp[1], tmp[0], tmp[0], ALU.mult).then_inc(step, 1)
                pool.wait_ge(step, base + 3)
                g.tensor_tensor(tmp[1], tmp[1], tmp[2], ALU.mult).then_inc(step, 1)
                pool.wait_ge(step, base + 4)
                g.tensor_tensor(tmp[1], tmp[1], threehalf[:, 0:n], ALU.add).then_inc(step, 1)
                pool.wait_ge(step, base + 5)
                return g.tensor_tensor(r, tmp[0], tmp[1], ALU.mult)

            def norm_x(t, p):
                g.tensor_tensor(xc[:, p, :], xa[:, t, :], ln1[:, 4, t].unsqueeze(1).broadcast_to([P, DIM]),
                                ALU.subtract).then_inc(xc_done, 1)
                pool.wait_ge(xc_done, t + 1)
                wait(pool, xT_filled, t - 1)
                g.tensor_tensor(xn[:, p, :], xc[:, p, :], ln1[:, 6, t].unsqueeze(1).broadcast_to([P, DIM]),
                                ALU.mult).then_inc(xn_ready, 1)
                g.tensor_tensor(xa[:, t, :], xa[:, t, :], boutb[:], ALU.add).then_inc(xb_ready, 1)

            def deviations(L, t0, t1, step, base, done):
                rsqrt(L[:, 5, t0:t1], L[:, 6, t0:t1], (L[:, 1, t0:t1], L[:, 3, t0:t1], L[:, 7, t0:t1]), step, base)\
                    .then_inc(done, 1)

            pool.wait_ge(var1_ready, 1)
            deviations(ln1, 0, 2, r1_step, 0, r1_ready)
            pool.wait_ge(wa_loaded, W_A)
            pool.wait_ge(r1_ready, 1)
            for t in range(2):
                norm_x(t, t)
            pool.wait_ge(var1_ready, 2)
            deviations(ln1, 2, TILES, r1_step, 5, r1_ready)
            pool.wait_ge(r1_ready, 2)
            with pool.Fori(1, TILES // 2) as i:
                for p in range(2):
                    norm_x(i * 2 + p, p)

            pool.wait_ge(var_ready, 1)
            deviations(ln2, 0, TILES, r2_step, 0, r2_ready)

            def affine(t, p):
                pool.wait_ge(z_ready, t + 1)
                g.tensor_tensor(xl[:, p, :], xl[:, p, :], gammab[:], ALU.mult).then_inc(aff_step, 1)
                pool.wait_ge(aff_step, t + 1)
                g.tensor_tensor(xl[:, p, :], xl[:, p, :], betab[:], ALU.add).then_inc(xl_ready, 1)

            def row_scale(t, p):
                s = sm2[:, p, :]
                pool.wait_ge(ss_clamped, t + 1)
                rsqrt(s[:, 0:1], s[:, 3:4], (s[:, 1:2], s[:, 2:3], s[:, 4:5]), rn_step, t * 6).then_inc(rn_step, 1)
                pool.wait_ge(rn_step, t * 6 + 6)
                wait(pool, e_ready, (t - 1) * 4)
                g.tensor_tensor(rn[:, p:p + 1], s[:, 3:4], scaleb[:], ALU.mult).then_inc(rn_ready, 1)

            pool.wait_ge(wb_loaded, W_B)
            affine(0, 0)
            row_scale(0, 0)
            affine(1, 1)
            for t in range(2):
                row_scale(t + 1, 1 - t)
                affine(t + 2, t)
            with pool.Fori(1, TILES // 2 - 1) as i:
                for p in range(2):
                    row_scale(i * 2 + p + 1, 1 - p)
                    affine(i * 2 + p + 2, p)
            row_scale(TILES - 1, 1)

        @block.scalar
        def _(act):
            a = nc.scalar
            act.wait_ge(ang_ready, 1)
            a.activation(ang[:], ang[:], ACT.Sin).then_inc(sin_ready, 1)
            act.wait_ge(mu_loaded, 16)
            musq = pb[:].rearrange("p a g h k -> p (a g h k)")
            a.activation(musq, mun[:].rearrange("p k n -> p (k n)"), ACT.Square).then_inc(musq_ready, 1)
            for c in range(4):
                act.wait_ge(muss_ready, c + 1)
                a.activation(pT[:].rearrange("p a b -> p (a b)")[:, c * BANK:(c + 1) * BANK], bank[c][:],
                             ACT.Sqrt).then_inc(munorm_ready, 1)

            def exps(t, p):
                for gr in range(GROUPS):
                    act.wait_ge(sub_done, t * 4 + gr + 1)
                    a.activation(pb[:, p, gr], pb[:, p, gr], ACT.Exp, scale=HD ** -0.5).then_inc(p_ready, 1)

            def pT_copy(t):
                for gr in (0, 2):
                    act.wait_ge(pT_filled, t * 4 + gr + 1)
                    a.copy(pT[:, 4 * gr:4 * gr + 4, :].rearrange("p a b -> p (a b)"), bank[6][:]).then_inc(pT_act, 1)

            def v_copy(t, p):
                act.wait_ge(v_filled, t + 1)
                for b in range(2):
                    for j in range(2):
                        src = bank[3][64 * b:64 * b + 64, 0:DIM].rearrange(
                            "p (m r j d) -> p r m j d", m=8, r=2, j=2)[:, :, :, j, :]
                        dst = vb[64 * j:64 * j + 64, p, b, :, 0:256].rearrange(
                            "p r (m c) -> p r m c", c=32)[:, :, :, 8 * j:8 * j + 8]
                        a.copy(dst, src).then_inc(v_ready, 1)

            def kq_copy(t):
                for half in range(2):
                    act.wait_ge(kq_filled, t * 3 + half + 1)
                    a.copy(kT[:, half], bank[half][:].rearrange("p (j n) -> p j n", j=4)).then_inc(kq_ready, 1)
                act.wait_ge(kq_filled, t * 3 + 3)
                a.copy(qT[:], bank[2][:, 0:DIM].rearrange("p (j n) -> p j n", j=2)).then_inc(kq_ready, 1)

            def step(s, p, before=True, after=True):
                exps(s, p)
                if before:
                    pT_copy(s - 1)
                if after:
                    v_copy(s + 1, 1 - p)
                    kq_copy(s + 1)

            act.wait_ge(consts_dve, 8)
            v_copy(0, 0)
            kq_copy(0)
            act.wait_ge(mu_ready, 2)
            step(0, 0, before=False)
            step(1, 1)
            with act.Fori(1, TILES // 2 - 1) as i:
                for p in range(2):
                    step(i * 2 + p, p)
            step(TILES - 2, 0)
            step(TILES - 1, 1, after=False)
            pT_copy(TILES - 1)

            def sumsq(t, p):
                act.wait_ge(xl_ready, t + 1)
                a.activation(sq[:], xl[:, p, :], ACT.Square, accum_out=ss[:, p:p + 1]).then_inc(ss_ready, 1)

            def slot_exps(t, p):
                act.wait_ge(rn_ready, t + 1)
                wait(act, es_ready, t)
                for c in range(4):
                    act.wait_ge(l_filled, t * 4 + c + 1)
                    a.activation(eb[:, 4 * c:4 * c + 4, :].rearrange("p a b -> p (a b)"), bank[c % 2][:], ACT.Exp,
                                 scale=rn[:, p:p + 1], bias=nshift[:]).then_inc(e_ready, 1)

            def eT_copy(t):
                for gr in (0, 2):
                    act.wait_ge(eT_filled, t * 4 + gr + 1)
                    a.copy(eT[:, 4 * gr:4 * gr + 4, :].rearrange("p a b -> p (a b)"), bank[6][:]).then_inc(eT_act, 1)

            def gelus(t):
                for i, (e0, e1) in enumerate(GG):
                    act.wait_ge(hn_ready, t * len(HG) + min(2 * i + 2, len(HG)))
                    a.activation(hb[:, e0:e1], hb[:, e0:e1], ACT.Gelu).then_inc(h_ready, 1)

            def gT_copy(t):
                act.wait_ge(g_filled, t * 2 + 1)
                a.copy(gT[:, 0:4, :].rearrange("p a b -> p (a b)"), bank[3][:]).then_inc(gT_act, 1)

            def ffn_step(s, p, last=False, sums=True):
                eT_copy(s)
                gelus(s)
                if not last:
                    slot_exps(s + 1, 1 - p)
                gT_copy(s)
                if sums:
                    sumsq(s + 2, p)

            act.wait_ge(shift_ready, 1)
            sumsq(0, 0)
            slot_exps(0, 0)
            sumsq(1, 1)
            with act.Fori(0, TILES // 2 - 1) as i:
                for p in range(2):
                    ffn_step(i * 2 + p, p)
            ffn_step(TILES - 2, 0, sums=False)
            ffn_step(TILES - 1, 1, last=True, sums=False)

        @block.vector
        def _(dve):
            v = nc.vector
            v.memset(kz[:].rearrange("p a b -> p (a b)"), 0.0).then_inc(consts_dve, 1)
            v.memset(vb[:].rearrange("p a b c d -> p (a b c d)"), 0.0).then_inc(consts_dve, 1)
            v.memset(xw[:].rearrange("p a b -> p (a b)"), 0.0).then_inc(consts_dve, 1)
            v.memset(hone[:].rearrange("p a b -> p (a b)"), 0.0).then_inc(consts_dve, 1)
            dve.wait_ge(consts_dve, 4)
            for b in range(2):
                v.memset(xw[64 * b:64 * b + 64, :, b * HC + HID:b * HC + HC], 1.0).then_inc(consts_dve, 1)
                hv = hone[64 * b:64 * b + 64].rearrange("p r (q j d) -> p r q j d", q=2, j=2)
                for r in range(2):
                    m = v.memset(hv[:, r, r, b, :], 1.0)
                m.then_inc(consts_dve, 1)

            def moments(st, L, t0, t1, var_scale, var_bias, step, base, done):
                L = [L[:, i, t0:t1] for i in range(8)]
                st = [st[:, t0:t1, i] for i in range(6)]
                v.tensor_tensor(L[0], st[1], st[4], ALU.add).then_inc(step, 1)
                v.tensor_tensor(L[1], st[1], st[4], ALU.subtract).then_inc(step, 1)
                v.tensor_tensor(L[2], st[2], st[5], ALU.add).then_inc(step, 1)
                dve.wait_ge(step, base + 3)
                v.tensor_scalar(L[4], L[0], 0.5, None, ALU.mult).then_inc(step, 1)
                v.tensor_tensor(L[3], L[1], L[1], ALU.mult).then_inc(step, 1)
                dve.wait_ge(step, base + 5)
                v.tensor_scalar(L[3], L[3], DIM / 4.0, None, ALU.mult).then_inc(step, 1)
                dve.wait_ge(step, base + 6)
                v.tensor_tensor(L[2], L[2], L[3], ALU.add).then_inc(step, 1)
                dve.wait_ge(step, base + 7)
                v.tensor_scalar(L[5], L[2], var_scale / DIM, var_bias, ALU.mult, ALU.add).then_inc(done, 1)

            dve.wait_ge(x_loaded[0], 16)
            for t in range(2):
                v.bn_stats(st1[:, t, :], xa[:, t, :]).then_inc(st1_ready, 1)
            dve.wait_ge(st1_ready, 2)
            moments(st1, ln1, 0, 2, 1.0, LN_EPS, var1_step, 0, var1_ready)

            PI = 3.141592653589793
            PI32 = 3.1415925
            TURN_HI, ROUND = 6.28125, 12582912.0
            TURN_LO = 2 * PI - TURN_HI
            dve.wait_ge(pos_loaded, 16)
            for f in range(2):
                v.tensor_scalar(ang[:, 1, :, :, f], posb[:], ROPE_FREQ[f], None, ALU.mult).then_inc(ang_step, 1)
            dve.wait_ge(ang_step, 2)
            v.tensor_scalar(ang[:, 0], ang[:, 1], PI / 2, None, ALU.add).then_inc(ang_step, 1)
            dve.wait_ge(ang_step, 3)
            v.tensor_scalar(turns[:], ang[:], 1 / (2 * PI), ROUND, ALU.mult, ALU.add).then_inc(ang_step, 1)
            dve.wait_ge(ang_step, 4)
            v.tensor_scalar(turns[:], turns[:], ROUND, None, ALU.subtract).then_inc(ang_step, 1)
            dve.wait_ge(ang_step, 5)
            af, tf = (z[:].rearrange("p a t c f -> p (a t c f)") for z in (ang, turns))
            v.scalar_tensor_tensor(out=af, in0=tf, scalar=-TURN_HI, in1=af, op0=ALU.mult, op1=ALU.add)\
                .then_inc(ang_step, 1)
            dve.wait_ge(ang_step, 6)
            v.scalar_tensor_tensor(out=af, in0=tf, scalar=-TURN_LO, in1=af, op0=ALU.mult, op1=ALU.add)\
                .then_inc(ang_step, 1)
            dve.wait_ge(ang_step, 7)
            v.tensor_scalar(af, af, PI32, -PI32, ALU.min, ALU.max).then_inc(ang_ready, 1)
            dve.wait_ge(sin_ready, 1)
            for e in range(2):
                dst = cosb[:].rearrange("p t (c f e) -> p t c f e", c=2, f=2)[:, :, :, :, e]
                v.tensor_copy(dst.rearrange("p t c f -> p (t c) f"), ang[:, 0].rearrange("p t c f -> p (t c) f"))\
                    .then_inc(rope_ready, 1)
                dst = sinb[:].rearrange("p t (c f e) -> p t c f e", c=2, f=2)[:, :, :, :, e]
                v.tensor_scalar(dst.rearrange("p t c f -> p (t c) f"), ang[:, 1].rearrange("p t c f -> p (t c) f"),
                                1.0 - 2.0 * e, None, ALU.mult).then_inc(rope_ready, 1)

            def xT_copy(t):
                dve.wait_ge(xT_filled, t + 1)
                v.tensor_copy(xT[:].rearrange("p a b -> p (a b)"), bank[4][:, 0:3 * P]).then_inc(xT_ready, 1)

            def rope(t):
                dve.wait_ge(qk_filled, t + 1)
                src = bank[5][:].rearrange("p (h c) -> p h c", c=8)
                v.tensor_tensor(ra[:], src, cosb[:, t, :].unsqueeze(1).broadcast_to([P, 64, 8]), ALU.mult)\
                    .then_inc(ropeab_done, 1)
                v.tensor_tensor(rb[:], src, sinb[:, t, :].unsqueeze(1).broadcast_to([P, 64, 8]), ALU.mult)\
                    .then_inc(ropeab_done, 1)
                dve.wait_ge(ropeab_done, t * 2 + 2)
                for e in range(2):
                    v.tensor_tensor(qr[:].rearrange("p (n e) -> p n e", e=2)[:, :, e],
                                    ra[:, 0:32].rearrange("p h (c e) -> p (h c) e", e=2)[:, :, e],
                                    rb[:, 0:32].rearrange("p h (c e) -> p (h c) e", e=2)[:, :, 1 - e],
                                    ALU.add).then_inc(qk_roped, 1)
                    for half in range(2):
                        dst = kz[:, half].rearrange("p (j r) -> p j r", j=4)[:, :, 0:128].rearrange(
                            "p j (g q) -> p j g q", q=32)[:, :, :, 0:8].rearrange(
                            "p j g (c e) -> p j g c e", e=2)[:, :, :, :, e]
                        ka, kb = (z[:, 32 + 16 * half:48 + 16 * half].rearrange(
                            "p (g j) (c e) -> p j g c e", j=4, e=2) for z in (ra, rb))
                        v.tensor_tensor(dst, ka[:, :, :, :, e], kb[:, :, :, :, 1 - e], ALU.add)\
                            .then_inc(qk_roped, 1)

            def softmax_max(t, gr):
                dve.wait_ge(s_filled, t * 4 + gr + 1)
                v.reduce_max(mx[:, gr, :], bank[gr][:].rearrange("p (h k) -> p h k", k=SEQ), AX.X)\
                    .then_inc(max_done, 1)

            def softmax_sub(t, p, gr):
                dve.wait_ge(max_done, t * 4 + gr + 1)
                v.tensor_tensor(pb[:, p, gr], bank[gr][:].rearrange("p (h k) -> p h k", k=SEQ),
                                mx[:, gr, :].unsqueeze(2).broadcast_to([P, 8, SEQ]), ALU.subtract)\
                    .then_inc(sub_done, 1)

            def softmax(t, p):
                softmax_max(t, 0)
                for gr in range(1, GROUPS):
                    softmax_max(t, gr)
                    softmax_sub(t, p, gr - 1)
                softmax_sub(t, p, GROUPS - 1)

            def pT_copy(t):
                for gr in (1, 3):
                    dve.wait_ge(pT_filled, t * 4 + gr + 1)
                    v.tensor_copy(pT[:, 4 * gr:4 * gr + 4, :].rearrange("p a b -> p (a b)"), bank[7][:])\
                        .then_inc(pT_dve, 1)

            def normalise(t):
                dve.wait_ge(o_filled, t + 1)
                v.reciprocal(rc[:], bank[4][:, DIM:2 * DIM]).then_inc(rc_done, 1)
                dve.wait_ge(rc_done, t + 1)
                v.tensor_tensor(oT[:], bank[4][:, 0:DIM], rc[:], ALU.mult).then_inc(oT_ready, 1)

            def residual(t):
                dve.wait_ge(a_filled, t + 1)
                dve.wait_ge(xb_ready, t + 1)
                v.tensor_tensor(xa[:, t, :], bank[5][:, 0:DIM], xa[:, t, :], ALU.add).then_inc(x1_ready, 1)
                dve.wait_ge(x1_ready, t + 1)
                v.bn_stats(st2[:, t, :], xa[:, t, :]).then_inc(st2_ready, 1)

            def step(s, p, before=True, after=True):
                softmax(s, p)
                if after:
                    xT_copy(s + 1)
                if before:
                    pT_copy(s - 1)
                if after:
                    rope(s + 1)
                if before:
                    normalise(s - 1)
                    residual(s - 1)

            xT_copy(0)
            dve.wait_ge(rope_ready, 4)
            dve.wait_ge(consts_dve, 8)
            rope(0)
            dve.wait_ge(x_loaded[1], 16)
            with dve.Fori(2, TILES) as t:
                v.bn_stats(st1[:, t, :], xa[:, t, :]).then_inc(st1_ready, 1)
            dve.wait_ge(st1_ready, TILES)
            moments(st1, ln1, 2, TILES, 1.0, LN_EPS, var1_step, 7, var1_ready)
            rmu = pT[:].rearrange("p a b -> p (a b)")
            dve.wait_ge(munorm_ready, 4)
            v.tensor_scalar(rmu, rmu, L2_EPS, None, ALU.max).then_inc(mu_step, 1)
            dve.wait_ge(mu_step, 1)
            v.reciprocal(rmu, rmu).then_inc(mu_step, 1)
            dve.wait_ge(mu_step, 2)
            for k in range(KD):
                v.tensor_tensor(mun[:, k, :], mun[:, k, :], rmu, ALU.mult).then_inc(mu_ready, 1)
            dve.wait_ge(wa_loaded, W_A)
            v.tensor_scalar(nshift[:], scaleb[:], -1.0, None, ALU.mult).then_inc(shift_step, 1)
            dve.wait_ge(shift_step, 1)
            v.tensor_tensor(nshift[:], nshift[:], scaleb[:], ALU.min).then_inc(shift_step, 1)
            dve.wait_ge(shift_step, 2)
            v.tensor_scalar(nshift[:], nshift[:], SAFE, 0.0, ALU.add, ALU.min).then_inc(shift_ready, 1)

            step(0, 0, before=False)
            step(1, 1)
            with dve.Fori(1, TILES // 2 - 1) as i:
                for p in range(2):
                    step(i * 2 + p, p)
            step(TILES - 2, 0)
            step(TILES - 1, 1, after=False)
            pT_copy(TILES - 1)
            normalise(TILES - 1)
            residual(TILES - 1)

            dve.wait_ge(st2_ready, TILES)
            moments(st2, ln2, 0, TILES, 1 + LN_EPS, LN_EPS * LN_EPS, var_step, 0, var_ready)

            def center(t, p):
                wait(dve, xlT_filled, t - 1)
                v.tensor_scalar(xl[:, p, :], xa[:, t, :], ln2[:, 4, t].unsqueeze(1), ln2[:, 6, t].unsqueeze(1),
                                ALU.subtract, ALU.mult).then_inc(z_ready, 1)

            def clamp(t, p):
                dve.wait_ge(ss_ready, t + 1)
                wait(dve, rn_ready, t - 1)
                v.tensor_scalar(sm2[:, p, 0:1], ss[:, p:p + 1], L2_EPS * L2_EPS, None, ALU.max)\
                    .then_inc(ss_clamped, 1)

            def xlT_copy(t):
                dve.wait_ge(xlT_filled, t + 1)
                v.tensor_copy(xlT[:].rearrange("p a b -> p (a b)"), bank[2][:, 0:DIM]).then_inc(xlT_ready, 1)

            def xw_copy(t):
                for c in range(2):
                    dve.wait_ge(xw_filled, t * 2 + c + 1)
                    for b in range(2):
                        rows = slice(64 * b, 64 * b + 64)
                        v.tensor_tensor(xw[rows, 8 * c:8 * c + 8, b * HC:b * HC + HID],
                                        bank[2 + c][rows].rearrange("p (e h) -> p e h", h=HID),
                                        b1b[rows, 8 * c:8 * c + 8, :], ALU.add).then_inc(xw_ready, 1)

            def eT_copy(t, gr):
                dve.wait_ge(eT_filled, t * 4 + gr + 1)
                v.tensor_copy(eT[:, 4 * gr:4 * gr + 4, :].rearrange("p a b -> p (a b)"), bank[7][:])\
                    .then_inc(eT_dve, 1)

            def sums(t):
                wait(dve, esT_filled, t)
                dve.wait_ge(e_ready, t * 4 + 4)
                v.reduce_sum(es[:], eb[:], AX.X).then_inc(es_ready, 1)
                dve.wait_ge(es_ready, t + 1)
                v.reduce_sum(rs[:, 0:1], es[:], AX.X).then_inc(rs_step, 1)
                dve.wait_ge(rs_step, t * 2 + 1)
                v.reciprocal(rs[:, 1:2], rs[:, 0:1]).then_inc(rs_step, 1)

            def hidden(t):
                for i, gr in enumerate(HG):
                    n, e0 = len(gr), gr[0]
                    dve.wait_ge(h_filled, t * len(HG) + i + 1)
                    src = bank[4 + i % 2][:, 0:n * 2 * HC].rearrange("p (n b c) -> p n b c", b=2, c=HC)
                    v.reciprocal(rh[:, e0:e0 + n, :], src[:, :, :, HID]).then_inc(rh_done, 1)
                    dve.wait_ge(rh_done, t * len(HG) + i + 1)
                    v.tensor_tensor(hb[:, e0:e0 + n], src[:, :, :, 0:HID],
                                    rh[:, e0:e0 + n, :].unsqueeze(3).broadcast_to([P, n, 2, HID]),
                                    ALU.mult).then_inc(hn_ready, 1)

            def gT_copy(t):
                dve.wait_ge(esT_filled, t + 1)
                v.tensor_copy(esT[:], bank[7][0:EXPERTS, 0:P]).then_inc(esT_ready, 1)
                dve.wait_ge(g_filled, t * 2 + 2)
                v.tensor_copy(gT[:, 4:8, :].rearrange("p a b -> p (a b)"), bank[6][:]).then_inc(gT_dve, 1)

            def finish(t, p):
                dve.wait_ge(y_filled, t + 1)
                dve.wait_ge(rs_step, t * 2 + 2)
                if not isinstance(t, int) or t >= 2:
                    dve.wait_ge(stored[p], (t - p) * 8)
                v.scalar_tensor_tensor(out=yo[:, p, :], in0=bank[4][:, 0:DIM], scalar=rs[:, 1:2], in1=xa[:, t, :],
                                       op0=ALU.mult, op1=ALU.add).then_inc(yo_ready, 1)

            def ffn_step(s, p, last=False, ahead=True):
                if not last:
                    clamp(s + 1, 1 - p)
                xw_copy(s)
                eT_copy(s, 1)
                sums(s)
                eT_copy(s, 3)
                hidden(s)
                if not last:
                    xlT_copy(s + 1)
                if ahead:
                    center(s + 2, p)
                gT_copy(s)
                finish(s, p)

            dve.wait_ge(r2_ready, 1)
            center(0, 0)
            center(1, 1)
            dve.wait_ge(wb_loaded, W_B)
            clamp(0, 0)
            xlT_copy(0)
            ffn_step(0, 0)
            ffn_step(1, 1)
            with dve.Fori(1, TILES // 2 - 1) as i:
                for p in range(2):
                    ffn_step(i * 2 + p, p)
            ffn_step(TILES - 2, 0, ahead=False)
            ffn_step(TILES - 1, 1, last=True, ahead=False)

        @block.tensor
        def _(pe):
            mm = nc.tensor.matmul
            pe.wait_ge(consts_pool, 4)

            def transpose_x(t, p):
                pe.wait_ge(xn_ready, t + 1)
                pe.wait_ge(ctx_loaded[p], (t - p) * 8 + 16)
                wait(pe, oT_ready, t - 2)
                for k in range(KD):
                    nc.tensor.transpose(bank[4][:, k * P:(k + 1) * P], xn[:, p, k * P:(k + 1) * P], ident[:])
                nc.tensor.transpose(bank[4][:, 2 * P:3 * P], ctile[:, p, :], ident[:]).then_inc(xT_filled, 1)

            def project_qk(t):
                pe.wait_ge(xT_ready, t + 1)
                wait(pe, x1_ready, t - 2)
                for k in range(KD):
                    mm(bank[5][:, 0:DIM], xT[:, k, :], wq[:, k, :], start=(k == 0), stop=(k == KD - 1))
                mm(bank[5][:, DIM:2 * DIM], xT[:, 2, :], wkv[:, 0:DIM], start=True, stop=True).then_inc(qk_filled, 1)

            def project_v(t):
                wait(pe, sub_done, t * 4)
                mm(bank[3][:, 0:DIM], xT[:, 2, :], wkv[:, DIM:2 * DIM], start=True, stop=True).then_inc(v_filled, 1)

            def transpose_kq(t):
                pe.wait_ge(qk_roped, t * 6 + 6)
                for half in range(2):
                    for j in range(4):
                        m = nc.tensor.transpose(bank[half][:, j * P:(j + 1) * P], kz[:, half, j * P:(j + 1) * P],
                                                ident[:])
                    m.then_inc(kq_filled, 1)
                for k in range(KD):
                    m = nc.tensor.transpose(bank[2][:, k * P:(k + 1) * P], qr[:, k * P:(k + 1) * P], ident[:])
                m.then_inc(kq_filled, 1)

            def logits(t):
                pe.wait_ge(kq_ready, t * 3 + 3)
                pe.wait_ge(v_ready, t * 4 + 4)
                for g0 in (0, 2):
                    for half in range(2):
                        for b in range(2):
                            for g in (g0, g0 + 1):
                                rows, cols = slice(32 * g, 32 * g + 32), slice(64 * b, 64 * b + 64)
                                m = mm(bank[g][cols, 256 * half:256 * half + 256].rearrange("p (j n) -> p j n", j=4),
                                       qT[rows, half, cols], kT[rows, half, :, cols], start=True, stop=True)
                                if half and b:
                                    m.then_inc(s_filled, 1)

            def transpose_p(t, p):
                for gr in range(GROUPS):
                    pe.wait_ge(p_ready, t * 4 + gr + 1)
                    if gr < 2:
                        wait(pe, (pT_act, pT_dve)[gr], t * 2)
                    else:
                        pe.wait_ge((pT_act, pT_dve)[gr - 2], t * 2 + 1)
                    for i in range(4):
                        m = nc.tensor.transpose(bank[6 + gr % 2][:, i * P:(i + 1) * P],
                                                pb[:, p, gr, 2 * i:2 * i + 2, :].rearrange("p h k -> p (h k)"),
                                                ident[:])
                    m.then_inc(pT_filled, 1)

            def attend(t, p):
                pe.wait_ge(pT_act, t * 2 + 2)
                pe.wait_ge(pT_dve, t * 2 + 2)
                pe.wait_ge(v_ready, t * 4 + 4)
                for half in range(2):
                    for b in range(2):
                        for what in range(2):
                            for r in range(2):
                                for g in range(GROUPS):
                                    m_ = half * GROUPS + g
                                    c = 256 * r + 32 * m_
                                    lhs = hone[:, r, :] if what else \
                                        vb[:, p, b].rearrange("p r c -> p (r c)")[:, c:c + 32]
                                    c = what * DIM + half * P + b * 64
                                    m = mm(bank[4][32 * g:32 * g + 32, c:c + 64], lhs,
                                           pT[:, 4 * g + 2 * half + r, b * 64:b * 64 + 64],
                                           start=(r == 0), stop=(r == 1))
                m.then_inc(o_filled, 1)

            def project_out(t):
                pe.wait_ge(oT_ready, t + 1)
                for k in range(KD):
                    m = mm(bank[5][:, 0:DIM], oT[:, k * P:(k + 1) * P], wo[:, k, :], start=(k == 0), stop=(k == KD - 1))
                m.then_inc(a_filled, 1)

            def step(s, p, before=True, after=True):
                logits(s)
                if after:
                    transpose_x(s + 1, 1 - p)
                if before:
                    transpose_p(s - 1, 1 - p)
                if after:
                    project_qk(s + 1)
                if before:
                    attend(s - 1, 1 - p)
                if after:
                    project_v(s + 1)
                    transpose_kq(s + 1)
                if before:
                    project_out(s - 1)

            pe.wait_ge(musq_ready, 1)
            musq = pb[:].rearrange("p a g h k -> p (a g h k)")
            for c in range(4):
                for k in range(KD):
                    m = mm(bank[c][:], ones[:], musq[:, k * ES + c * BANK:k * ES + (c + 1) * BANK],
                           start=(k == 0), stop=(k == KD - 1))
                m.then_inc(muss_ready, 1)
            pe.wait_ge(wa_loaded, W_A)
            transpose_x(0, 0)
            project_qk(0)
            pe.wait_ge(munorm_ready, 4)
            project_v(0)
            transpose_kq(0)
            step(0, 0, before=False)
            step(1, 1)
            with pe.Fori(1, TILES // 2 - 1) as i:
                for p in range(2):
                    step(i * 2 + p, p)
            step(TILES - 2, 0)
            step(TILES - 1, 1, after=False)
            transpose_p(TILES - 1, 1)
            attend(TILES - 1, 1)
            project_out(TILES - 1)

            def transpose_xl(t, p):
                pe.wait_ge(xl_ready, t + 1)
                for k in range(KD):
                    m = nc.tensor.transpose(bank[2][:, k * P:(k + 1) * P], xl[:, p, k * P:(k + 1) * P], ident[:])
                m.then_inc(xlT_filled, 1)

            def slot_logits(t):
                pe.wait_ge(xlT_ready, t + 1)
                for c in range(4):
                    if c < 2:
                        wait(pe, e_ready, t * 4 - 1 + c)
                    else:
                        pe.wait_ge(e_ready, t * 4 + c - 1)
                    for k in range(KD):
                        m = mm(bank[c % 2][:], xlT[:, k, :], mun[:, k, c * BANK:(c + 1) * BANK],
                               start=(k == 0), stop=(k == KD - 1))
                    m.then_inc(l_filled, 1)

            def expand(t):
                for c in range(2):
                    for k in range(KD):
                        m = mm(bank[2 + c][:], xlT[:, k, :], w1[:, k, c * BANK:(c + 1) * BANK],
                               start=(k == 0), stop=(k == KD - 1))
                    m.then_inc(xw_filled, 1)

            def transpose_e(t):
                for gr in range(4):
                    pe.wait_ge(e_ready, t * 4 + gr + 1)
                    if gr >= 2:
                        pe.wait_ge((eT_act, eT_dve)[gr - 2], t * 2 + 1)
                    for i in range(4):
                        m = nc.tensor.transpose(bank[6 + gr % 2][:, i * P:(i + 1) * P], eb[:, 4 * gr + i, :], ident[:])
                    m.then_inc(eT_filled, 1)

            def dispatch(t):
                pe.wait_ge(xw_ready, t * 4 + 4)
                for i, gr in enumerate(HG):
                    if i == 0:
                        wait(pe, yo_ready, t)
                    if i >= 2:
                        pe.wait_ge(hn_ready, t * len(HG) + i - 1)
                    for n, e in enumerate(gr):
                        m = mm(bank[4 + i % 2][:, n * 2 * HC:(n + 1) * 2 * HC], eb[:, e, :], xw[:, e, :],
                               start=True, stop=True)
                    m.then_inc(h_filled, 1)

            def combine(t):
                pe.wait_ge(es_ready, t + 1)
                pe.wait_ge(eT_act, t * 2 + 2)
                pe.wait_ge(eT_dve, t * 2 + 2)
                nc.tensor.transpose(bank[7][0:EXPERTS, 0:P], es[:], ident[:]).then_inc(esT_filled, 1)
                pe.wait_ge(h_ready, t * len(GG) + len(GG))
                for c in range(2):
                    for i in range(4):
                        for b in range(2):
                            for r in range(2):
                                e = 8 * c + 2 * i + r
                                m = mm((bank[3], bank[6])[c][64 * r:64 * r + 64, i * P + b * 64:i * P + b * 64 + 64],
                                       hb[:, e, b, :], eT[:, e, b * 64:b * 64 + 64], start=True, stop=True)
                    m.then_inc(g_filled, 1)

            def contract(t):
                pe.wait_ge(esT_ready, t + 1)
                mm(bank[4][:, 0:DIM], esT[:], b2s[:], start=True, stop=False)
                pe.wait_ge(gT_act, t + 1)
                for i in range(EXPERTS // 2):
                    if i == 4:
                        pe.wait_ge(gT_dve, t + 1)
                    m = mm(bank[4][:, 0:DIM], gT[:, i, :], w2[:, i, :], start=False, stop=(i == EXPERTS // 2 - 1))
                m.then_inc(y_filled, 1)

            def ffn_step(s, p, last=False):
                expand(s)
                transpose_e(s)
                dispatch(s)
                if not last:
                    transpose_xl(s + 1, 1 - p)
                    slot_logits(s + 1)
                combine(s)
                contract(s)

            pe.wait_ge(wb_loaded, W_B)
            transpose_xl(0, 0)
            slot_logits(0)
            ffn_step(0, 0)
            ffn_step(1, 1)
            with pe.Fori(1, TILES // 2 - 1) as i:
                for p in range(2):
                    ffn_step(i * 2 + p, p)
            ffn_step(TILES - 2, 0)
            ffn_step(TILES - 1, 1, last=True)


_INS = ['x', 'ctx_1024', 'fside_BxSx2_0', 'L0_xattn_Wq', 'L0_xattn_Wkv', 'L0_xattn_Wout', 'L0_xattn_bout',
        'L0_ffn_gamma', 'L0_ffn_beta', 'L0_ffn_mu', 'L0_ffn_scale', 'L0_ffn_W1', 'L0_ffn_b1', 'L0_ffn_W2',
        'L0_ffn_b2']


def kernel(**inputs):
    import numpy as _np
    import concourse.bacc as _bacc
    from concourse import mybir as _mybir
    from concourse.bass_utils import run_bass_kernel_spmd as _run

    nc = _bacc.Bacc("TRN2", target_bir_lowering=False, num_devices=1)
    arrays, args = {}, []
    for name in _INS:
        a = _np.ascontiguousarray(inputs[name])
        arrays[f"in_{name}"] = a
        args.append(nc.dram_tensor(f"in_{name}", a.shape, _mybir.dt.from_np(a.dtype), kind="ExternalInput").ap())
    out = nc.dram_tensor("out", (BATCH, SEQ, DIM), F32, kind="ExternalOutput").ap()
    build(nc, *args, out)
    r = _run(nc, [arrays], core_ids=[0])
    return r.results[0]["out"]
```

```python
import concourse.bass as bass
from concourse import mybir
from contextlib import ExitStack

F32 = mybir.dt.float32
F32R = mybir.dt.float32r
ALU = mybir.AluOpType
ACT = mybir.ActivationFunctionType
AX = mybir.AxisListType

P = 128
BATCH, SEQ, DIM, CDIM = 32, 64, 256, 128
TILES = BATCH * SEQ // P
KD = DIM // P
HEADS, HD = 32, 8
EXPERTS, SLOTS, HID = 16, 128, 64
ES = EXPERTS * SLOTS
AHEAD = 4
BANK = 512
LN_EPS = 1e-5
L2_EPS = 1e-12
ROPE_FREQ = (1.0, 0.01)
SAFE = 80.0
GROUPS = 4
HC = HID + 1


def wait(eng, sem, value):
    if isinstance(value, int) and value <= 0:
        return
    eng.wait_ge(sem, value)


def build(nc, x, ctx_in, pos, Wq, Wkv, Wout, bout, gamma, beta, mu, scale, W1, b1, W2, b2, out):
    ctx = ExitStack()
    with ctx:
        def sb(name, *shape, dt=F32):
            return ctx.enter_context(nc.sbuf_tensor(name, list(shape), dt))

        def split(name, *shape):
            return sb(name + "_h", *shape, dt=F32R), sb(name + "_l", *shape, dt=F32R)

        def sem(name):
            return ctx.enter_context(nc.semaphore(name))

        ident = sb("ident", P, P)
        ones = sb("ones", P, P)
        wqkv = split("wqkv", P, KD + 2, DIM)
        wo = sb("wo", P, KD, DIM)
        mu_raw = sb("mu_raw", P, KD, ES)
        mun = split("mun", P, KD, ES)
        w12_raw = sb("w12_raw", P, 2, ES)
        w1 = split("w1", P, KD, EXPERTS * HID)
        w2 = split("w2", P, EXPERTS // 2, DIM)
        mu_r = sb("mu_r", P, 5, EXPERTS)
        b2s = sb("b2s", EXPERTS, DIM)
        boutb = sb("boutb", P, DIM)
        scaleb = sb("scaleb", P, 1)
        nshift = sb("nshift", P, 1)
        posb = sb("posb", P, TILES, 2)
        ang = sb("ang", P, 2, TILES, 2, 2)
        turns = sb("turns", P, 2, TILES, 2, 2)
        cosb = sb("cosb", P, TILES, 8)
        sinb = sb("sinb", P, TILES, 8)
        mhalf = sb("mhalf", P, TILES)
        threehalf = sb("threehalf", P, TILES)
        hone = sb("hone", P, 2, 32)

        xa = sb("xa", P, TILES, DIM)
        ctile = sb("ctile", P, 2, CDIM)
        st1 = sb("st1", P, TILES, 6)
        ln1 = sb("ln1", P, 8, TILES)
        xc = sb("xc", P, 2, DIM)
        xn = sb("xn", P, 2, DIM)
        xT = split("xT", P, 3, P)
        ra = sb("ra", P, 64, 8)
        rb = sb("rb", P, 64, 8)
        qr = sb("qr", P, DIM)
        kz = sb("kz", P, 2, 544)
        qT = sb("qT", P, 2, P)
        kT = sb("kT", P, 2, 4, P)
        vb = sb("vb", P, 2, 2, 2, 272)
        mx = sb("mx", P, GROUPS, 8)
        pb = sb("pb", P, 2, GROUPS, 8, SEQ)
        pT = sb("pT", P, 16, P)
        rc = sb("rc", P, DIM)
        oT = sb("oT", P, DIM)
        st2 = sb("st2", P, TILES, 6)
        ln2 = sb("ln2", P, 8, TILES)
        ss = sb("ss", P, 2)
        sm2 = sb("sm2", P, 2, 8)
        rn = sb("rn", P, 2)
        xlT = split("xlT", P, KD, P)
        eb = sb("eb", P, EXPERTS, SLOTS)
        es = sb("es", P, EXPERTS)
        rs = sb("rs", P, 2, 2)
        rh = sb("rh", P, EXPERTS, 2)
        gT = split("gT", P, EXPERTS // 2, P)
        esT = sb("esT", EXPERTS, P)

        bank = [ctx.enter_context(nc.psum_tensor(f"bank{i}", [P, BANK], F32)) for i in range(8)]

        x_loaded = [sem("x_loaded0"), sem("x_loaded1")]
        wqkv_loaded = sem("wqkv_loaded")
        small_loaded = sem("small_loaded")
        wo_loaded = sem("wo_loaded")
        pos_loaded = sem("pos_loaded")
        mu_loaded = sem("mu_loaded")
        w12_loaded = sem("w12_loaded")
        wb_loaded = sem("wb_loaded")
        ctx_loaded = [sem("ctx_loaded0"), sem("ctx_loaded1")]
        ident_step = sem("ident_step")
        consts_pool = sem("consts_pool")
        consts_dve = sem("consts_dve")
        ang_step = sem("ang_step")
        ang_ready = sem("ang_ready")
        sin_ready = sem("sin_ready")
        rope_ready = sem("rope_ready")
        musq_ready = sem("musq_ready")
        muss_ready = sem("muss_ready")
        muss_clamped = sem("muss_clamped")
        mur_step = sem("mur_step")
        mur_ready = sem("mur_ready")
        diag_ready = sem("diag_ready")
        rb_filled = sem("rb_filled")
        rb_ready = sem("rb_ready")
        muscale_step = sem("muscale_step")
        split_step = sem("split_step")
        w12_ready = sem("w12_ready")
        mu_ready = sem("mu_ready")
        wqkv_step = sem("wqkv_step")
        wqkv_ready = sem("wqkv_ready")
        shift_step = sem("shift_step")
        shift_ready = sem("shift_ready")
        st1_ready = sem("st1_ready")
        var1_step = sem("var1_step")
        var1_ready = sem("var1_ready")
        r1_step = sem("r1_step")
        r1_ready = sem("r1_ready")
        xc_done = sem("xc_done")
        xn_ready = sem("xn_ready")
        xb_ready = sem("xb_ready")
        xT_filled = sem("xT_filled")
        xT_split = sem("xT_split")
        xT_ready = sem("xT_ready")
        qk_filled = sem("qk_filled")
        v_filled = sem("v_filled")
        ropeab_done = sem("ropeab_done")
        qk_roped = sem("qk_roped")
        v_ready = sem("v_ready")
        kq_filled = sem("kq_filled")
        kq_ready = sem("kq_ready")
        s_filled = sem("s_filled")
        max_done = sem("max_done")
        sub_done = sem("sub_done")
        p_ready = sem("p_ready")
        pT_filled = sem("pT_filled")
        pT_ready = sem("pT_ready")
        o_filled = sem("o_filled")
        rc_done = sem("rc_done")
        oT_ready = sem("oT_ready")
        a_filled = sem("a_filled")
        x1_ready = sem("x1_ready")
        st2_ready = sem("st2_ready")
        var_step = sem("var_step")
        var_ready = sem("var_ready")
        r2_step = sem("r2_step")
        r2_ready = sem("r2_ready")
        z_ready = sem("z_ready")
        aff_step = sem("aff_step")
        xl_ready = sem("xl_ready")
        ss_ready = sem("ss_ready")
        ss_clamped = sem("ss_clamped")
        rn_step = sem("rn_step")
        rn_ready = sem("rn_ready")
        xlT_filled = sem("xlT_filled")
        xlT_split = sem("xlT_split")
        xlT_ready = sem("xlT_ready")
        l_filled = sem("l_filled")
        e_ready = sem("e_ready")
        xw_step = sem("xw_step")
        xw_const = sem("xw_const")
        xw_filled = sem("xw_filled")
        xw_ready = sem("xw_ready")
        eT_filled = sem("eT_filled")
        eT_act = sem("eT_act")
        eT_dve = sem("eT_dve")
        es_ready = sem("es_ready")
        h_filled = sem("h_filled")
        rh_done = sem("rh_done")
        hn_ready = sem("hn_ready")
        h_ready = sem("h_ready")
        g_filled = sem("g_filled")
        gT_split = sem("gT_split")
        gT_ready = sem("gT_ready")
        esT_filled = sem("esT_filled")
        esT_ready = sem("esT_ready")
        rs_step = sem("rs_step")
        y_filled = sem("y_filled")
        yo_ready = sem("yo_ready")
        stored = [sem("stored0"), sem("stored1")]

        x_d = x.rearrange("b s d -> (b s) d").rearrange("(t p) d -> p t d", p=P)
        ctx_d = ctx_in.rearrange("b s d -> (b s) d").rearrange("(t p) d -> p t d", p=P)
        pos_d = pos.rearrange("b s c -> (b s) c").rearrange("(t p) c -> p t c", p=P)
        out_d = out.rearrange("b s d -> (b s) d").rearrange("(t p) d -> p t d", p=P)

        def row(v, n):
            return v.rearrange("(a d) -> a d", a=1).broadcast_to([P, n])

        PER = BANK // (2 * HC)
        HG = [range(i, min(i + PER, EXPERTS)) for i in range(0, EXPERTS, PER)]
        GG = [(HG[i][0], HG[min(i + 1, len(HG) - 1)][-1] + 1) for i in range(0, len(HG), 2)]
        LB = (0, 1, 2, 5)
        HB = (4, 5, 3)

        def flat(t):
            return t[:].rearrange("p a b -> p (a b)")

        wqkv_raw = flat(pT)[:, 0:(KD + 2) * DIM].rearrange("p (k n) -> p k n", n=DIM)
        w1_raw, w2_raw = w12_raw[:, 0, :], w12_raw[:, 1, :]
        musq = [flat(eb), w12_raw[:, 0, :]]
        diag = w12_raw[:, 1, :].rearrange("p (e s) -> p e s", s=P)
        mu_rb = flat(eb)
        eT = mu_raw[:, 0, :].rearrange("p (e s) -> p e s", s=P)
        b1b = mu_raw[:, 1, 0:EXPERTS * HID].rearrange("p (e h) -> p e h", h=HID)
        gammab = mu_raw[:, 1, 1024:1024 + DIM]
        betab = mu_raw[:, 1, 1024 + DIM:1024 + 2 * DIM]
        w12f = flat(w12_raw)
        XW = EXPERTS * 2 * HC
        xw = w12f[:, 0:XW].rearrange("p (e c) -> p e c", c=2 * HC)
        yo = w12f[:, XW:XW + 2 * DIM].rearrange("p (a d) -> p a d", d=DIM)
        sq = w12f[:, XW + 2 * DIM:XW + 3 * DIM]
        hb = pb[:, 1].rearrange("p g h k -> p (g h k)").rearrange("p (e b h) -> p e b h", b=2, h=HID)
        xl = xc

        block = ctx.enter_context(nc.Block())

        @block.sync
        def _(sp):
            def load_ctx(t, p):
                wait(sp, xT_filled, t - 1)
                sp.dma_start(ctile[:, p, :], ctx_d[:, t, :]).then_inc(ctx_loaded[p], 16)

            def store(t, p):
                sp.wait_ge(yo_ready, t + 1)
                sp.dma_start(out_d[:, t, :], yo[:, p, :]).then_inc(stored[p], 16)

            sp.dma_start(xa[:, 0:AHEAD, :], x_d[:, 0:AHEAD, :]).then_inc(x_loaded[0], 16)
            load_ctx(0, 0)
            sp.dma_start(wqkv_raw[:, 0:KD, :], Wq.rearrange("(k p) n -> p k n", p=P)).then_inc(wqkv_loaded, 16)
            sp.dma_start(wqkv_raw[:, KD:KD + 2, :], Wkv.rearrange("p (k n) -> p k n", k=2)).then_inc(wqkv_loaded, 16)
            sp.dma_start(posb[:], pos_d).then_inc(pos_loaded, 16)
            sp.dma_start(boutb[:], row(bout, DIM)).then_inc(small_loaded, 16)
            sp.dma_start(scaleb[:], row(scale, 1)).then_inc(small_loaded, 16)
            load_ctx(1, 1)
            sp.dma_start(xa[:, AHEAD:TILES, :], x_d[:, AHEAD:TILES, :]).then_inc(x_loaded[1], 16)
            sp.dma_start(wo[:], Wout.rearrange("(k p) n -> p k n", p=P)).then_inc(wo_loaded, 16)
            sp.dma_start(mu_raw[:], mu.rearrange("(k p) e s -> p k (e s)", p=P)).then_inc(mu_loaded, 16)
            with sp.Fori(1, 5) as i:
                for p in range(2):
                    load_ctx(i * 2 + p, p)
            sp.wait_ge(rb_filled, 4)
            for k in range(KD):
                sp.dma_start(w1_raw[:, k * 1024:(k + 1) * 1024].rearrange("p (e h) -> p e h", h=HID),
                             W1[:, k * P:(k + 1) * P, :].rearrange("e p h -> p e h")).then_inc(w12_loaded, 16)
            sp.dma_start(w2_raw.rearrange("p (k d) -> p k d", d=DIM),
                         W2.rearrange("e h d -> (e h) d").rearrange("(k p) d -> p k d", p=P)).then_inc(w12_loaded, 16)
            with sp.Fori(5, TILES // 2) as i:
                for p in range(2):
                    load_ctx(i * 2 + p, p)
            sp.wait_ge(mu_ready, 2)
            sp.dma_start(b1b.rearrange("p e h -> p (e h)"), row(b1.rearrange("e h -> (e h)"), EXPERTS * HID))\
                .then_inc(wb_loaded, 16)
            sp.dma_start(b2s[:], b2).then_inc(wb_loaded, 16)
            sp.dma_start(gammab, row(gamma, DIM)).then_inc(wb_loaded, 16)
            sp.dma_start(betab, row(beta, DIM)).then_inc(wb_loaded, 16)
            with sp.Fori(0, TILES // 2) as i:
                for p in range(2):
                    store(i * 2 + p, p)
            for p in range(2):
                sp.wait_ge(stored[p], 16 * TILES // 2)

        @block.gpsimd
        def _(pool):
            g = nc.gpsimd
            g.memset(ident[:], 0.0).then_inc(ident_step, 1)
            pool.wait_ge(ident_step, 1)
            g.affine_select(out=ident[:], in_=ident[:], compare_op=ALU.not_equal, fill=1.0, base=0,
                            pattern=[[-1, P]], channel_multiplier=1).then_inc(consts_pool, 1)
            g.memset(mhalf[:], -0.5).then_inc(consts_pool, 1)
            g.memset(ones[:], 1.0).then_inc(consts_pool, 1)
            g.memset(threehalf[:], 1.5).then_inc(consts_pool, 1)
            pool.wait_ge(consts_pool, 4)

            def rsqrt(a, r, tmp, step, base):
                n = r.shape[1]
                g.tensor_tensor(tmp[0], a, mhalf[:, 0:n], ALU.pow).then_inc(step, 1)
                g.tensor_tensor(tmp[2], a, mhalf[:, 0:n], ALU.mult).then_inc(step, 1)
                pool.wait_ge(step, base + 1)
                g.tensor_tensor(tmp[1], tmp[0], tmp[0], ALU.mult).then_inc(step, 1)
                pool.wait_ge(step, base + 3)
                g.tensor_tensor(tmp[1], tmp[1], tmp[2], ALU.mult).then_inc(step, 1)
                pool.wait_ge(step, base + 4)
                g.tensor_tensor(tmp[1], tmp[1], threehalf[:, 0:n], ALU.add).then_inc(step, 1)
                pool.wait_ge(step, base + 5)
                return g.tensor_tensor(r, tmp[0], tmp[1], ALU.mult)

            def norm_x(t, p):
                g.tensor_tensor(xc[:, p, :], xa[:, t, :], ln1[:, 4, t].unsqueeze(1).broadcast_to([P, DIM]),
                                ALU.subtract).then_inc(xc_done, 1)
                pool.wait_ge(xc_done, t + 1)
                wait(pool, xT_filled, t - 1)
                g.tensor_tensor(xn[:, p, :], xc[:, p, :], ln1[:, 6, t].unsqueeze(1).broadcast_to([P, DIM]),
                                ALU.mult).then_inc(xn_ready, 1)
                g.tensor_tensor(xa[:, t, :], xa[:, t, :], boutb[:], ALU.add).then_inc(xb_ready, 1)

            def deviations(L, t0, t1, step, base, done):
                rsqrt(L[:, 5, t0:t1], L[:, 6, t0:t1], (L[:, 1, t0:t1], L[:, 3, t0:t1], L[:, 7, t0:t1]), step, base)\
                    .then_inc(done, 1)

            def split_pool(raw, halves, base, done):
                high, low = halves
                g.tensor_copy(high, raw).then_inc(split_step, 1)
                pool.wait_ge(split_step, base + 1)
                g.tensor_tensor(low, raw, high.bitcast(F32), ALU.subtract).then_inc(done, 1)

            pool.wait_ge(var1_ready, 1)
            deviations(ln1, 0, AHEAD, r1_step, 0, r1_ready)
            pool.wait_ge(small_loaded, 32)
            pool.wait_ge(r1_ready, 1)
            for t in range(AHEAD):
                norm_x(t, t % 2)
            pool.wait_ge(var1_ready, 2)
            deviations(ln1, AHEAD, TILES, r1_step, 5, r1_ready)
            pool.wait_ge(r1_ready, 2)
            pool.wait_ge(mu_loaded, 16)
            for k in range(KD):
                g.tensor_tensor(musq[k], mu_raw[:, k, :], mu_raw[:, k, :], ALU.mult).then_inc(musq_ready, 1)
            pool.wait_ge(musq_ready, 2)
            g.tensor_tensor(musq[0], musq[0], musq[1], ALU.add).then_inc(musq_ready, 1)
            with pool.Fori(2, 3) as i:
                for p in range(2):
                    norm_x(i * 2 + p, p)
            pool.wait_ge(muss_clamped, 1)
            R = [mu_r[:, i, :] for i in range(5)]
            rsqrt(R[0], R[1], (R[2], R[3], R[4]), mur_step, 0).then_inc(mur_ready, 1)
            pool.wait_ge(mur_ready, 1)
            g.tensor_tensor(diag, ident[:].unsqueeze(1).broadcast_to([P, EXPERTS, P]),
                            R[1].unsqueeze(2).broadcast_to([P, EXPERTS, P]), ALU.mult).then_inc(diag_ready, 1)
            with pool.Fori(3, 5) as i:
                for p in range(2):
                    norm_x(i * 2 + p, p)
            pool.wait_ge(rb_ready, 4)
            for k in range(KD):
                with pool.Fori(5 + k, 6 + k) as i:
                    for p in range(2):
                        norm_x(i * 2 + p, p)
                g.tensor_tensor(mu_raw[:, k, :], mu_raw[:, k, :], mu_rb, ALU.mult).then_inc(muscale_step, 1)
                pool.wait_ge(muscale_step, k + 1)
                split_pool(mu_raw[:, k, :], [h[:, k, :] for h in mun], k, mu_ready)
            with pool.Fori(7, TILES // 2) as i:
                for p in range(2):
                    norm_x(i * 2 + p, p)
            pool.wait_ge(w12_loaded, 48)
            split_pool(w1_raw, [flat(h) for h in w1], 2, w12_ready)
            split_pool(w2_raw, [flat(h) for h in w2], 3, w12_ready)
            pool.wait_ge(w12_ready, 2)
            g.memset(w12f[:, 0:XW], 0.0).then_inc(xw_step, 1)
            pool.wait_ge(xw_step, 1)
            for b in range(2):
                g.memset(xw[64 * b:64 * b + 64, :, b * HC + HID:b * HC + HC], 1.0).then_inc(xw_const, 1)
            pool.wait_ge(xw_const, 2)

            pool.wait_ge(var_ready, 1)
            deviations(ln2, 0, TILES - 4, r2_step, 0, r2_ready)

            def affine(t, p):
                pool.wait_ge(z_ready, t + 1)
                g.tensor_tensor(xl[:, p, :], xl[:, p, :], gammab, ALU.mult).then_inc(aff_step, 1)
                pool.wait_ge(aff_step, t + 1)
                g.tensor_tensor(xl[:, p, :], xl[:, p, :], betab, ALU.add).then_inc(xl_ready, 1)

            def row_scale(t, p):
                s = sm2[:, p, :]
                pool.wait_ge(ss_clamped, t + 1)
                rsqrt(s[:, 0:1], s[:, 3:4], (s[:, 1:2], s[:, 2:3], s[:, 4:5]), rn_step, t * 6).then_inc(rn_step, 1)
                pool.wait_ge(rn_step, t * 6 + 6)
                wait(pool, e_ready, (t - 1) * 4)
                g.tensor_tensor(rn[:, p:p + 1], s[:, 3:4], scaleb[:], ALU.mult).then_inc(rn_ready, 1)

            pool.wait_ge(wb_loaded, 64)
            affine(0, 0)
            row_scale(0, 0)
            affine(1, 1)
            for t in range(2):
                row_scale(t + 1, 1 - t)
                affine(t + 2, t)
                if t == 0:
                    pool.wait_ge(var_ready, 2)
                    deviations(ln2, TILES - 4, TILES, r2_step, 5, r2_ready)
            with pool.Fori(1, TILES // 2 - 1) as i:
                for p in range(2):
                    row_scale(i * 2 + p + 1, 1 - p)
                    affine(i * 2 + p + 2, p)
            row_scale(TILES - 1, 1)

        @block.scalar
        def _(act):
            a = nc.scalar
            act.wait_ge(ang_ready, 1)
            a.activation(ang[:], ang[:], ACT.Sin).then_inc(sin_ready, 1)
            act.wait_ge(wqkv_loaded, 32)
            a.copy(flat(wqkv[0]), flat(wqkv_raw)).then_inc(wqkv_step, 1)

            def exp_group(t, p, gr):
                act.wait_ge(sub_done, t * 4 + gr + 1)
                a.activation(pb[:, p, gr], pb[:, p, gr], ACT.Exp, scale=HD ** -0.5).then_inc(p_ready, 1)

            def pT_copy(t, gr):
                act.wait_ge(pT_filled, t * 4 + gr + 1)
                a.copy(pT[:, 4 * gr:4 * gr + 4, :].rearrange("p a b -> p (a b)"), bank[6 + gr % 2][:])\
                    .then_inc(pT_ready, 1)

            def v_copy(t, p):
                act.wait_ge(v_filled, t + 1)
                wait(act, o_filled, t - 1)
                for b in range(2):
                    for j in range(2):
                        src = bank[6][64 * b:64 * b + 64, 0:DIM].rearrange(
                            "p (m r j d) -> p r m j d", m=8, r=2, j=2)[:, :, :, j, :]
                        dst = vb[64 * j:64 * j + 64, p, b, :, 0:256].rearrange(
                            "p r (m c) -> p r m c", c=32)[:, :, :, 8 * j:8 * j + 8]
                        a.copy(dst, src).then_inc(v_ready, 1)

            def kq_copy(t):
                for half in range(2):
                    act.wait_ge(kq_filled, t * 3 + half + 1)
                    a.copy(kT[:, half], bank[half][:].rearrange("p (j n) -> p j n", j=4)).then_inc(kq_ready, 1)
                act.wait_ge(kq_filled, t * 3 + 3)
                a.copy(qT[:], bank[2][:, 0:DIM].rearrange("p (j n) -> p j n", j=2)).then_inc(kq_ready, 1)

            def step(s, p, before=True, after=True):
                for g0 in (0, 2):
                    if before:
                        for gr in (g0, g0 + 1):
                            pT_copy(s - 1, gr)
                    for gr in (g0, g0 + 1):
                        exp_group(s, p, gr)
                if after:
                    kq_copy(s + 1)
                    v_copy(s + 1, 1 - p)

            act.wait_ge(consts_dve, 5)
            kq_copy(0)
            v_copy(0, 0)
            step(0, 0, before=False)
            step(1, 1)
            with act.Fori(1, 4) as i:
                for p in range(2):
                    step(i * 2 + p, p)
            for c in range(4):
                act.wait_ge(rb_filled, c + 1)
                a.copy(mu_rb[:, c * BANK:(c + 1) * BANK], bank[6 + c % 2][:]).then_inc(rb_ready, 1)
            with act.Fori(4, TILES // 2 - 1) as i:
                for p in range(2):
                    step(i * 2 + p, p)
            step(TILES - 2, 0)
            step(TILES - 1, 1, after=False)
            def sumsq(t, p):
                act.wait_ge(xl_ready, t + 1)
                a.activation(sq, xl[:, p, :], ACT.Square, accum_out=ss[:, p:p + 1]).then_inc(ss_ready, 1)

            def slot_exps(t, p):
                act.wait_ge(rn_ready, t + 1)
                wait(act, es_ready, t)
                for c in range(4):
                    act.wait_ge(l_filled, t * 4 + c + 1)
                    a.activation(eb[:, 4 * c:4 * c + 4, :].rearrange("p a b -> p (a b)"), bank[LB[c]][:], ACT.Exp,
                                 scale=rn[:, p:p + 1], bias=nshift[:]).then_inc(e_ready, 1)

            def eT_copy(t):
                for gr in (0, 2):
                    act.wait_ge(eT_filled, t * 4 + gr + 1)
                    a.copy(eT[:, 4 * gr:4 * gr + 4, :].rearrange("p a b -> p (a b)"),
                           bank[(6, 7, 0, 1)[gr]][:]).then_inc(eT_act, 1)

            def gelus(t):
                for i, (e0, e1) in enumerate(GG):
                    act.wait_ge(hn_ready, t * len(HG) + min(2 * i + 2, len(HG)))
                    a.activation(hb[:, e0:e1], hb[:, e0:e1], ACT.Gelu).then_inc(h_ready, 1)

            def gT_high(t):
                for c in range(2):
                    act.wait_ge(g_filled, t * 2 + c + 1)
                    a.copy(gT[0][:, 4 * c:4 * c + 4, :].rearrange("p a b -> p (a b)"), bank[(3, 6)[c]][:])\
                        .then_inc(gT_split, 1)

            def ffn_step(s, p, last=False, sums=True):
                eT_copy(s)
                gelus(s)
                if not last:
                    slot_exps(s + 1, 1 - p)
                gT_high(s)
                if sums:
                    sumsq(s + 2, p)

            act.wait_ge(shift_ready, 1)
            act.wait_ge(w12_ready, 2)
            sumsq(0, 0)
            slot_exps(0, 0)
            for gr in range(GROUPS):
                pT_copy(TILES - 1, gr)
            sumsq(1, 1)
            with act.Fori(0, TILES // 2 - 1) as i:
                for p in range(2):
                    ffn_step(i * 2 + p, p)
            ffn_step(TILES - 2, 0, sums=False)
            ffn_step(TILES - 1, 1, last=True, sums=False)

        @block.vector
        def _(dve):
            v = nc.vector
            v.memset(kz[:].rearrange("p a b -> p (a b)"), 0.0).then_inc(consts_dve, 1)
            v.memset(vb[:].rearrange("p a b c d -> p (a b c d)"), 0.0).then_inc(consts_dve, 1)
            v.memset(hone[:].rearrange("p a b -> p (a b)"), 0.0).then_inc(consts_dve, 1)
            dve.wait_ge(consts_dve, 3)
            for b in range(2):
                hv = hone[64 * b:64 * b + 64].rearrange("p r (q j d) -> p r q j d", q=2, j=2)
                for r in range(2):
                    m = v.memset(hv[:, r, r, b, :], 1.0)
                m.then_inc(consts_dve, 1)

            def moments(st, L, t0, t1, var_scale, var_bias, step, base, done):
                L = [L[:, i, t0:t1] for i in range(8)]
                st = [st[:, t0:t1, i] for i in range(6)]
                v.tensor_tensor(L[0], st[1], st[4], ALU.add).then_inc(step, 1)
                v.tensor_tensor(L[1], st[1], st[4], ALU.subtract).then_inc(step, 1)
                v.tensor_tensor(L[2], st[2], st[5], ALU.add).then_inc(step, 1)
                dve.wait_ge(step, base + 3)
                v.tensor_scalar(L[4], L[0], 0.5, None, ALU.mult).then_inc(step, 1)
                v.tensor_tensor(L[3], L[1], L[1], ALU.mult).then_inc(step, 1)
                dve.wait_ge(step, base + 5)
                v.tensor_scalar(L[3], L[3], DIM / 4.0, None, ALU.mult).then_inc(step, 1)
                dve.wait_ge(step, base + 6)
                v.tensor_tensor(L[2], L[2], L[3], ALU.add).then_inc(step, 1)
                dve.wait_ge(step, base + 7)
                v.tensor_scalar(L[5], L[2], var_scale / DIM, var_bias, ALU.mult, ALU.add).then_inc(done, 1)

            dve.wait_ge(x_loaded[0], 16)
            for t in range(AHEAD):
                v.bn_stats(st1[:, t, :], xa[:, t, :]).then_inc(st1_ready, 1)
            dve.wait_ge(st1_ready, AHEAD)
            moments(st1, ln1, 0, AHEAD, 1.0, LN_EPS, var1_step, 0, var1_ready)

            PI = 3.141592653589793
            PI32 = 3.1415925
            TURN_HI, ROUND = 6.28125, 12582912.0
            TURN_LO = 2 * PI - TURN_HI
            dve.wait_ge(pos_loaded, 16)
            for f in range(2):
                v.tensor_scalar(ang[:, 1, :, :, f], posb[:], ROPE_FREQ[f], None, ALU.mult).then_inc(ang_step, 1)
            dve.wait_ge(ang_step, 2)
            v.tensor_scalar(ang[:, 0], ang[:, 1], PI / 2, None, ALU.add).then_inc(ang_step, 1)
            dve.wait_ge(ang_step, 3)
            v.tensor_scalar(turns[:], ang[:], 1 / (2 * PI), ROUND, ALU.mult, ALU.add).then_inc(ang_step, 1)
            dve.wait_ge(ang_step, 4)
            v.tensor_scalar(turns[:], turns[:], ROUND, None, ALU.subtract).then_inc(ang_step, 1)
            dve.wait_ge(ang_step, 5)
            af, tf = (z[:].rearrange("p a t c f -> p (a t c f)") for z in (ang, turns))
            v.scalar_tensor_tensor(out=af, in0=tf, scalar=-TURN_HI, in1=af, op0=ALU.mult, op1=ALU.add)\
                .then_inc(ang_step, 1)
            dve.wait_ge(ang_step, 6)
            v.scalar_tensor_tensor(out=af, in0=tf, scalar=-TURN_LO, in1=af, op0=ALU.mult, op1=ALU.add)\
                .then_inc(ang_step, 1)
            dve.wait_ge(ang_step, 7)
            v.tensor_scalar(af, af, PI32, -PI32, ALU.min, ALU.max).then_inc(ang_ready, 1)

            def xT_copy(t):
                dve.wait_ge(xT_filled, t + 1)
                v.tensor_copy(flat(xT[0]), bank[7][:, 0:3 * P]).then_inc(xT_split, 1)
                dve.wait_ge(xT_split, t + 1)
                v.tensor_tensor(flat(xT[1]), bank[7][:, 0:3 * P], flat(xT[0]).bitcast(F32), ALU.subtract)\
                    .then_inc(xT_ready, 1)

            def rope_products(t):
                dve.wait_ge(qk_filled, t + 1)
                src = bank[4][:].rearrange("p (h c) -> p h c", c=8)
                v.tensor_tensor(ra[:], src, cosb[:, t, :].unsqueeze(1).broadcast_to([P, 64, 8]), ALU.mult)\
                    .then_inc(ropeab_done, 1)
                v.tensor_tensor(rb[:], src, sinb[:, t, :].unsqueeze(1).broadcast_to([P, 64, 8]), ALU.mult)\
                    .then_inc(ropeab_done, 1)

            def rope_sums(t):
                wait(dve, kq_filled, t * 3)
                dve.wait_ge(ropeab_done, t * 2 + 2)
                for e in range(2):
                    v.tensor_tensor(qr[:].rearrange("p (n e) -> p n e", e=2)[:, :, e],
                                    ra[:, 0:32].rearrange("p h (c e) -> p (h c) e", e=2)[:, :, e],
                                    rb[:, 0:32].rearrange("p h (c e) -> p (h c) e", e=2)[:, :, 1 - e],
                                    ALU.add).then_inc(qk_roped, 1)
                    for half in range(2):
                        dst = kz[:, half].rearrange("p (j r) -> p j r", j=4)[:, :, 0:128].rearrange(
                            "p j (g q) -> p j g q", q=32)[:, :, :, 0:8].rearrange(
                            "p j g (c e) -> p j g c e", e=2)[:, :, :, :, e]
                        ka, kb = (z[:, 32 + 16 * half:48 + 16 * half].rearrange(
                            "p (g j) (c e) -> p j g c e", j=4, e=2) for z in (ra, rb))
                        v.tensor_tensor(dst, ka[:, :, :, :, e], kb[:, :, :, :, 1 - e], ALU.add)\
                            .then_inc(qk_roped, 1)

            def softmax_max(t, gr):
                dve.wait_ge(s_filled, t * 4 + gr + 1)
                v.reduce_max(mx[:, gr, :], bank[gr][:].rearrange("p (h k) -> p h k", k=SEQ), AX.X)\
                    .then_inc(max_done, 1)

            def softmax_sub(t, p, gr):
                dve.wait_ge(max_done, t * 4 + gr + 1)
                v.tensor_tensor(pb[:, p, gr], bank[gr][:].rearrange("p (h k) -> p h k", k=SEQ),
                                mx[:, gr, :].unsqueeze(2).broadcast_to([P, 8, SEQ]), ALU.subtract)\
                    .then_inc(sub_done, 1)

            def softmax(t, p, g0):
                for gr in (g0, g0 + 1):
                    softmax_max(t, gr)
                for gr in (g0, g0 + 1):
                    softmax_sub(t, p, gr)

            def normalise(t):
                dve.wait_ge(o_filled, t + 1)
                v.reciprocal(rc[:], bank[4][:, DIM:2 * DIM]).then_inc(rc_done, 1)
                dve.wait_ge(rc_done, t + 1)
                v.tensor_tensor(oT[:], bank[4][:, 0:DIM], rc[:], ALU.mult).then_inc(oT_ready, 1)

            def residual(t, b=5):
                dve.wait_ge(a_filled, t + 1)
                dve.wait_ge(xb_ready, t + 1)
                v.tensor_tensor(xa[:, t, :], bank[b][:, 0:DIM], xa[:, t, :], ALU.add).then_inc(x1_ready, 1)
                dve.wait_ge(x1_ready, t + 1)
                v.bn_stats(st2[:, t, :], xa[:, t, :]).then_inc(st2_ready, 1)

            def step(s, p, before=True, after=True, out=True):
                if after:
                    xT_copy(s + 1)
                softmax(s, p, 0)
                if after:
                    rope_products(s + 1)
                softmax(s, p, 2)
                if after:
                    rope_sums(s + 1)
                if out:
                    residual(s - 2)
                if before:
                    normalise(s - 1)

            dve.wait_ge(wqkv_step, 1)
            v.tensor_tensor(flat(wqkv[1]), flat(wqkv_raw), flat(wqkv[0]).bitcast(F32), ALU.subtract)\
                .then_inc(wqkv_ready, 1)
            xT_copy(0)
            dve.wait_ge(sin_ready, 1)
            for e in range(2):
                dst = cosb[:].rearrange("p t (c f e) -> p t c f e", c=2, f=2)[:, :, :, :, e]
                v.tensor_copy(dst.rearrange("p t c f -> p (t c) f"), ang[:, 0].rearrange("p t c f -> p (t c) f"))\
                    .then_inc(rope_ready, 1)
                dst = sinb[:].rearrange("p t (c f e) -> p t c f e", c=2, f=2)[:, :, :, :, e]
                v.tensor_scalar(dst.rearrange("p t c f -> p (t c) f"), ang[:, 1].rearrange("p t c f -> p (t c) f"),
                                1.0 - 2.0 * e, None, ALU.mult).then_inc(rope_ready, 1)
            dve.wait_ge(rope_ready, 4)
            rope_products(0)
            xT_copy(1)
            rope_sums(0)
            dve.wait_ge(x_loaded[1], 16)
            for t in range(AHEAD, AHEAD + 4):
                v.bn_stats(st1[:, t, :], xa[:, t, :]).then_inc(st1_ready, 1)
            rope_products(1)
            rope_sums(1)
            dve.wait_ge(small_loaded, 32)
            v.tensor_scalar(nshift[:], scaleb[:], -1.0, None, ALU.mult).then_inc(shift_step, 1)
            dve.wait_ge(shift_step, 1)
            v.tensor_tensor(nshift[:], nshift[:], scaleb[:], ALU.min).then_inc(shift_step, 1)
            dve.wait_ge(shift_step, 2)
            v.tensor_scalar(nshift[:], nshift[:], SAFE, 0.0, ALU.add, ALU.min).then_inc(shift_ready, 1)

            softmax(0, 0, 0)
            softmax(0, 0, 2)
            with dve.Fori(AHEAD // 4 + 1, TILES // 4) as i:
                for u in range(4):
                    v.bn_stats(st1[:, i * 4 + u, :], xa[:, i * 4 + u, :]).then_inc(st1_ready, 1)
            dve.wait_ge(st1_ready, TILES)
            moments(st1, ln1, AHEAD, TILES, 1.0, LN_EPS, var1_step, 7, var1_ready)
            step(1, 1, out=False)
            with dve.Fori(1, 2) as i:
                for p in range(2):
                    step(i * 2 + p, p)
            dve.wait_ge(muss_ready, 1)
            v.tensor_scalar(mu_r[:, 0, :], bank[6][:, 0:EXPERTS], L2_EPS * L2_EPS, None, ALU.max)\
                .then_inc(muss_clamped, 1)
            with dve.Fori(2, TILES // 2 - 1) as i:
                for p in range(2):
                    step(i * 2 + p, p)
            dve.wait_ge(st2_ready, TILES - 4)
            moments(st2, ln2, 0, TILES - 4, 1 + LN_EPS, LN_EPS * LN_EPS, var_step, 0, var_ready)
            step(TILES - 2, 0)

            def center(t, p):
                wait(dve, xlT_filled, t - 1)
                v.tensor_scalar(xl[:, p, :], xa[:, t, :], ln2[:, 4, t].unsqueeze(1), ln2[:, 6, t].unsqueeze(1),
                                ALU.subtract, ALU.mult).then_inc(z_ready, 1)

            def clamp(t, p):
                dve.wait_ge(ss_ready, t + 1)
                wait(dve, rn_ready, t - 1)
                v.tensor_scalar(sm2[:, p, 0:1], ss[:, p:p + 1], L2_EPS * L2_EPS, None, ALU.max)\
                    .then_inc(ss_clamped, 1)

            def xlT_copy(t):
                dve.wait_ge(xlT_filled, t + 1)
                v.tensor_copy(flat(xlT[0]), bank[2][:, 0:DIM]).then_inc(xlT_split, 1)
                dve.wait_ge(xlT_split, t + 1)
                v.tensor_tensor(flat(xlT[1]), bank[2][:, 0:DIM], flat(xlT[0]).bitcast(F32), ALU.subtract)\
                    .then_inc(xlT_ready, 1)

            def xw_copy(t):
                for c in range(2):
                    dve.wait_ge(xw_filled, t * 2 + c + 1)
                    for b in range(2):
                        rows = slice(64 * b, 64 * b + 64)
                        v.tensor_tensor(xw[rows, 8 * c:8 * c + 8, b * HC:b * HC + HID],
                                        bank[2 + c][rows].rearrange("p (e h) -> p e h", h=HID),
                                        b1b[rows, 8 * c:8 * c + 8, :], ALU.add).then_inc(xw_ready, 1)

            def eT_copy(t, gr):
                dve.wait_ge(eT_filled, t * 4 + gr + 1)
                v.tensor_copy(eT[:, 4 * gr:4 * gr + 4, :].rearrange("p a b -> p (a b)"), bank[(6, 7, 0, 1)[gr]][:])\
                    .then_inc(eT_dve, 1)

            def sums(t, p):
                wait(dve, esT_filled, t)
                dve.wait_ge(e_ready, t * 4 + 4)
                v.reduce_sum(es[:], eb[:], AX.X).then_inc(es_ready, 1)
                dve.wait_ge(es_ready, t + 1)
                v.reduce_sum(rs[:, p, 0:1], es[:], AX.X).then_inc(rs_step, 1)
                dve.wait_ge(rs_step, t * 2 + 1)
                v.reciprocal(rs[:, p, 1:2], rs[:, p, 0:1]).then_inc(rs_step, 1)

            def hidden(t):
                for i, gr in enumerate(HG):
                    if i == 3:
                        eT_copy(t, 3)
                    n, e0 = len(gr), gr[0]
                    dve.wait_ge(h_filled, t * len(HG) + i + 1)
                    src = bank[HB[i % 3]][:, 0:n * 2 * HC].rearrange("p (n b c) -> p n b c", b=2, c=HC)
                    v.reciprocal(rh[:, e0:e0 + n, :], src[:, :, :, HID]).then_inc(rh_done, 1)
                    dve.wait_ge(rh_done, t * len(HG) + i + 1)
                    v.tensor_tensor(hb[:, e0:e0 + n], src[:, :, :, 0:HID],
                                    rh[:, e0:e0 + n, :].unsqueeze(3).broadcast_to([P, n, 2, HID]),
                                    ALU.mult).then_inc(hn_ready, 1)

            def gT_low(t):
                dve.wait_ge(esT_filled, t + 1)
                v.tensor_copy(esT[:], bank[7][0:EXPERTS, 0:P]).then_inc(esT_ready, 1)
                for c in range(2):
                    high, low = (h[:, 4 * c:4 * c + 4, :].rearrange("p a b -> p (a b)") for h in gT)
                    dve.wait_ge(gT_split, t * 2 + c + 1)
                    v.tensor_tensor(low, bank[(3, 6)[c]][:], high.bitcast(F32), ALU.subtract).then_inc(gT_ready, 1)

            def finish(t, p):
                dve.wait_ge(y_filled, t + 1)
                dve.wait_ge(rs_step, t * 2 + 2)
                if not isinstance(t, int) or t >= 2:
                    dve.wait_ge(stored[p], (t - p) * 8)
                v.scalar_tensor_tensor(out=yo[:, p, :], in0=bank[4][:, 0:DIM], scalar=rs[:, p, 1:2], in1=xa[:, t, :],
                                       op0=ALU.mult, op1=ALU.add).then_inc(yo_ready, 1)

            def ffn_step(s, p, last=False, ahead=True):
                if not last:
                    clamp(s + 1, 1 - p)
                xw_copy(s)
                if not last:
                    xlT_copy(s + 1)
                hidden(s)
                eT_copy(s, 1)
                if ahead:
                    center(s + 2, p)
                gT_low(s)
                if not last:
                    sums(s + 1, 1 - p)
                finish(s, p)

            dve.wait_ge(r2_ready, 1)
            center(0, 0)
            center(1, 1)
            softmax(TILES - 1, 1, 0)
            softmax(TILES - 1, 1, 2)
            residual(TILES - 3)
            xlT_copy(0)
            clamp(0, 0)
            normalise(TILES - 2)
            residual(TILES - 2, 3)
            dve.wait_ge(wb_loaded, 64)
            dve.wait_ge(xw_const, 2)
            sums(0, 0)
            normalise(TILES - 1)
            residual(TILES - 1, 6)
            dve.wait_ge(st2_ready, TILES)
            moments(st2, ln2, TILES - 4, TILES, 1 + LN_EPS, LN_EPS * LN_EPS, var_step, 7, var_ready)
            ffn_step(0, 0)
            ffn_step(1, 1)
            dve.wait_ge(r2_ready, 2)
            with dve.Fori(1, TILES // 2 - 1) as i:
                for p in range(2):
                    ffn_step(i * 2 + p, p)
            ffn_step(TILES - 2, 0, ahead=False)
            ffn_step(TILES - 1, 1, last=True, ahead=False)

        @block.tensor
        def _(pe):
            mm = nc.tensor.matmul
            pe.wait_ge(consts_pool, 4)

            def mm3(o, a, b, first=True, last=True):
                mm(o, a[1], b[0], start=first, stop=False)
                mm(o, a[0], b[1], start=False, stop=False)
                return mm(o, a[0], b[0], start=False, stop=last)

            def transpose_x(t, p):
                pe.wait_ge(xn_ready, t + 1)
                pe.wait_ge(ctx_loaded[p], (t - p) * 8 + 16)
                wait(pe, xT_ready, t)
                wait(pe, pT_ready, (t - 2) * 4)
                for k in range(KD):
                    nc.tensor.transpose(bank[7][:, k * P:(k + 1) * P], xn[:, p, k * P:(k + 1) * P], ident[:])
                nc.tensor.transpose(bank[7][:, 2 * P:3 * P], ctile[:, p, :], ident[:]).then_inc(xT_filled, 1)

            def project_qk(t):
                pe.wait_ge(xT_ready, t + 1)
                wait(pe, oT_ready, t - 2)
                for k in range(KD):
                    mm3(bank[4][:, 0:DIM], [h[:, k, :] for h in xT], [h[:, k, :] for h in wqkv],
                        first=(k == 0), last=(k == KD - 1))
                mm3(bank[4][:, DIM:2 * DIM], [h[:, KD, :] for h in xT], [h[:, KD, :] for h in wqkv])\
                    .then_inc(qk_filled, 1)

            def project_v(t):
                wait(pe, v_ready, t * 4)
                wait(pe, pT_ready, (t - 1) * 4)
                mm3(bank[6][:, 0:DIM], [h[:, KD, :] for h in xT], [h[:, KD + 1, :] for h in wqkv])\
                    .then_inc(v_filled, 1)

            def transpose_kq(t):
                pe.wait_ge(qk_roped, t * 6 + 6)
                for half in range(2):
                    wait(pe, sub_done, t * 4 - 3 + half)
                    for j in range(4):
                        m = nc.tensor.transpose(bank[half][:, j * P:(j + 1) * P], kz[:, half, j * P:(j + 1) * P],
                                                ident[:])
                    m.then_inc(kq_filled, 1)
                wait(pe, sub_done, t * 4 - 1)
                for k in range(KD):
                    m = nc.tensor.transpose(bank[2][:, k * P:(k + 1) * P], qr[:, k * P:(k + 1) * P], ident[:])
                m.then_inc(kq_filled, 1)

            def logits(t, g0, half):
                pe.wait_ge(kq_ready, t * 3 + 3)
                wait(pe, sub_done, t * 4)
                for b in range(2):
                    for g in (g0, g0 + 1):
                        rows, cols = slice(32 * g, 32 * g + 32), slice(64 * b, 64 * b + 64)
                        m = mm(bank[g][cols, 256 * half:256 * half + 256].rearrange("p (j n) -> p j n", j=4),
                               qT[rows, half, cols], kT[rows, half, :, cols], start=True, stop=True)
                        if half and b:
                            m.then_inc(s_filled, 1)

            def transpose_p(t, p, gr, more=True):
                pe.wait_ge(p_ready, t * 4 + gr + 1)
                if gr == 0:
                    wait(pe, v_ready, t * 4 + 8 if more else TILES * 4)
                if gr == 1 and more:
                    pe.wait_ge(xT_ready, t + 3)
                if gr >= 2:
                    pe.wait_ge(pT_ready, t * 4 + gr - 1)
                for i in range(4):
                    m = nc.tensor.transpose(bank[6 + gr % 2][:, i * P:(i + 1) * P],
                                            pb[:, p, gr, 2 * i:2 * i + 2, :].rearrange("p h k -> p (h k)"),
                                            ident[:])
                m.then_inc(pT_filled, 1)

            def attend(t, p, roped=True):
                pe.wait_ge(pT_ready, t * 4 + 4)
                pe.wait_ge(v_ready, t * 4 + 4)
                if roped:
                    pe.wait_ge(ropeab_done, t * 2 + 6)
                else:
                    pe.wait_ge(oT_ready, t)
                for half in range(2):
                    for b in range(2):
                        for what in range(2):
                            for r in range(2):
                                for g in range(GROUPS):
                                    m_ = half * GROUPS + g
                                    c = 256 * r + 32 * m_
                                    lhs = hone[:, r, :] if what else \
                                        vb[:, p, b].rearrange("p r c -> p (r c)")[:, c:c + 32]
                                    c = what * DIM + half * P + b * 64
                                    m = mm(bank[4][32 * g:32 * g + 32, c:c + 64], lhs,
                                           pT[:, 4 * g + 2 * half + r, b * 64:b * 64 + 64],
                                           start=(r == 0), stop=(r == 1))
                m.then_inc(o_filled, 1)

            def project_out(t, k, b=5):
                if k == 0:
                    pe.wait_ge(oT_ready, t + 1)
                    wait(pe, x1_ready, t)
                m = mm(bank[b][:, 0:DIM], oT[:, k * P:(k + 1) * P], wo[:, k, :], start=(k == 0), stop=(k == KD - 1))
                if k == KD - 1:
                    m.then_inc(a_filled, 1)

            def step(s, p, before=True, after=True, out=True, more=True):
                if after and before:
                    transpose_x(s + 1, 1 - p)
                logits(s, 0, 0)
                if before:
                    transpose_p(s - 1, 1 - p, 0, more=after)
                logits(s, 0, 1)
                if before:
                    transpose_p(s - 1, 1 - p, 1, more=after)
                if after and before:
                    project_qk(s + 1)
                logits(s, 2, 0)
                if before:
                    transpose_p(s - 1, 1 - p, 2)
                if out:
                    project_out(s - 2, 0)
                if before:
                    transpose_p(s - 1, 1 - p, 3)
                logits(s, 2, 1)
                if out:
                    project_out(s - 2, 1)
                if after:
                    if before:
                        attend(s - 1, 1 - p)
                    transpose_kq(s + 1)
                    project_v(s + 1)

            transpose_x(0, 0)
            pe.wait_ge(wqkv_ready, 1)
            project_qk(0)
            project_v(0)
            transpose_x(1, 1)
            transpose_kq(0)
            project_qk(1)
            step(0, 0, before=False, out=False)
            step(1, 1, out=False)
            pe.wait_ge(wo_loaded, 16)
            with pe.Fori(1, 2) as i:
                for p in range(2):
                    step(i * 2 + p, p)
            pe.wait_ge(musq_ready, 3)
            pe.wait_ge(v_ready, 20)
            for e in range(EXPERTS):
                m = mm(bank[6][:, e:e + 1], musq[0][:, e * SLOTS:(e + 1) * SLOTS], ones[:, 0:1], start=True, stop=True)
            m.then_inc(muss_ready, 1)
            pe.wait_ge(muss_clamped, 1)
            with pe.Fori(2, 4) as i:
                for p in range(2):
                    step(i * 2 + p, p)
            pe.wait_ge(diag_ready, 1)
            pe.wait_ge(v_ready, 36)
            for c in range(4):
                if c >= 2:
                    pe.wait_ge(rb_ready, c - 1)
                mm(bank[6 + c % 2][:], ones[:], diag[:, 4 * c:4 * c + 4, :].rearrange("p e s -> p (e s)"),
                   start=True, stop=True).then_inc(rb_filled, 1)
            pe.wait_ge(rb_ready, 4)
            with pe.Fori(4, TILES // 2 - 1) as i:
                for p in range(2):
                    step(i * 2 + p, p)
            step(TILES - 2, 0)
            def transpose_xl(t, p):
                pe.wait_ge(xl_ready, t + 1)
                wait(pe, xw_ready, t * 4 - 2)
                for k in range(KD):
                    m = nc.tensor.transpose(bank[2][:, k * P:(k + 1) * P], xl[:, p, k * P:(k + 1) * P], ident[:])
                m.then_inc(xlT_filled, 1)

            def slot_logits(t):
                pe.wait_ge(xlT_ready, t + 1)
                for c in range(4):
                    if c < 2:
                        wait(pe, (eT_act, eT_dve)[c], (t * 2, t * 2 - 1)[c])
                    elif c == 3:
                        wait(pe, hn_ready, (t - 1) * len(HG) + 5)
                    for k in range(KD):
                        m = mm3(bank[LB[c]][:], [h[:, k, :] for h in xlT],
                                [h[:, k, c * BANK:(c + 1) * BANK] for h in mun], first=(k == 0), last=(k == KD - 1))
                    m.then_inc(l_filled, 1)

            def expand(t):
                pe.wait_ge(e_ready, t * 4 + 3)
                for c in range(2):
                    for k in range(KD):
                        m = mm3(bank[2 + c][:], [h[:, k, :] for h in xlT],
                                [h[:, k, c * BANK:(c + 1) * BANK] for h in w1], first=(k == 0), last=(k == KD - 1))
                    m.then_inc(xw_filled, 1)

            def transpose_e(t):
                for gr in range(4):
                    pe.wait_ge(e_ready, t * 4 + gr + 1)
                    for i in range(4):
                        m = nc.tensor.transpose(bank[(6, 7, 0, 1)[gr]][:, i * P:(i + 1) * P], eb[:, 4 * gr + i, :],
                                                ident[:])
                    m.then_inc(eT_filled, 1)

            def dispatch(t):
                pe.wait_ge(xw_ready, t * 4 + 4)
                for i, gr in enumerate(HG):
                    if i == 0:
                        wait(pe, yo_ready, t)
                    if i >= 3:
                        pe.wait_ge(hn_ready, t * len(HG) + i - 2)
                    for n, e in enumerate(gr):
                        m = mm(bank[HB[i % 3]][:, n * 2 * HC:(n + 1) * 2 * HC], eb[:, e, :], xw[:, e, :],
                               start=True, stop=True)
                    m.then_inc(h_filled, 1)

            def combine(t):
                pe.wait_ge(es_ready, t + 1)
                pe.wait_ge(eT_act, t * 2 + 2)
                pe.wait_ge(eT_dve, t * 2 + 2)
                nc.tensor.transpose(bank[7][0:EXPERTS, 0:P], es[:], ident[:]).then_inc(esT_filled, 1)
                pe.wait_ge(h_ready, t * len(GG) + len(GG))
                for c in range(2):
                    for i in range(4):
                        for b in range(2):
                            for r in range(2):
                                e = 8 * c + 2 * i + r
                                m = mm((bank[3], bank[6])[c][64 * r:64 * r + 64, i * P + b * 64:i * P + b * 64 + 64],
                                       hb[:, e, b, :], eT[:, e, b * 64:b * 64 + 64], start=True, stop=True)
                    m.then_inc(g_filled, 1)

            def contract(t):
                pe.wait_ge(esT_ready, t + 1)
                mm(bank[4][:, 0:DIM], esT[:], b2s[:], start=True, stop=False)
                for i in range(EXPERTS // 2):
                    pe.wait_ge(gT_ready, t * 2 + i // 4 + 1)
                    m = mm3(bank[4][:, 0:DIM], [h[:, i, :] for h in gT], [h[:, i, :] for h in w2],
                            first=False, last=(i == EXPERTS // 2 - 1))
                m.then_inc(y_filled, 1)

            def ffn_step(s, p, last=False, expanded=False):
                if not expanded:
                    expand(s)
                transpose_e(s)
                if not last:
                    transpose_xl(s + 1, 1 - p)
                dispatch(s)
                if not last:
                    slot_logits(s + 1)
                combine(s)
                contract(s)

            pe.wait_ge(wb_loaded, 64)
            pe.wait_ge(mu_ready, 2)
            pe.wait_ge(w12_ready, 2)
            step(TILES - 1, 1, after=False)
            pe.wait_ge(sub_done, TILES * 4)
            transpose_xl(0, 0)
            attend(TILES - 2, 0, roped=False)
            pe.wait_ge(x1_ready, TILES - 2)
            slot_logits(0)
            for gr in range(GROUPS):
                transpose_p(TILES - 1, 1, gr, more=False)
                if gr % 2:
                    project_out(TILES - 2, gr // 2, 3)
            attend(TILES - 1, 1, roped=False)
            pe.wait_ge(x1_ready, TILES - 1)
            expand(0)
            for k in range(KD):
                project_out(TILES - 1, k, 6)
            pe.wait_ge(x1_ready, TILES)
            ffn_step(0, 0, expanded=True)
            ffn_step(1, 1)
            with pe.Fori(1, TILES // 2 - 1) as i:
                for p in range(2):
                    ffn_step(i * 2 + p, p)
            ffn_step(TILES - 2, 0)
            ffn_step(TILES - 1, 1, last=True)


_INS = ['x', 'ctx_1024', 'fside_BxSx2_0', 'L0_xattn_Wq', 'L0_xattn_Wkv', 'L0_xattn_Wout', 'L0_xattn_bout',
        'L0_ffn_gamma', 'L0_ffn_beta', 'L0_ffn_mu', 'L0_ffn_scale', 'L0_ffn_W1', 'L0_ffn_b1', 'L0_ffn_W2',
        'L0_ffn_b2']


def kernel(**inputs):
    import numpy as _np
    import concourse.bacc as _bacc
    from concourse import mybir as _mybir
    from concourse.bass_utils import run_bass_kernel_spmd as _run

    nc = _bacc.Bacc("TRN2", target_bir_lowering=False, num_devices=1)
    arrays, args = {}, []
    for name in _INS:
        a = _np.ascontiguousarray(inputs[name])
        arrays[f"in_{name}"] = a
        args.append(nc.dram_tensor(f"in_{name}", a.shape, _mybir.dt.from_np(a.dtype), kind="ExternalInput").ap())
    out = nc.dram_tensor("out", (BATCH, SEQ, DIM), F32, kind="ExternalOutput").ap()
    build(nc, *args, out)
    r = _run(nc, [arrays], core_ids=[0])
    return r.results[0]["out"]
```

```python
import concourse.bass as bass
from concourse import mybir
from contextlib import ExitStack

F32 = mybir.dt.float32
F32R = mybir.dt.float32r
ALU = mybir.AluOpType
ACT = mybir.ActivationFunctionType
AX = mybir.AxisListType

P = 128
BATCH, SEQ, DIM, CDIM = 32, 64, 256, 128
TILES = BATCH * SEQ // P
KD = DIM // P
HEADS, HD = 32, 8
EXPERTS, SLOTS, HID = 16, 128, 64
ES = EXPERTS * SLOTS
AHEAD = 4
BANK = 512
LN_EPS = 1e-5
L2_EPS = 1e-12
ROPE_FREQ = (1.0, 0.01)
SAFE = 80.0
GROUPS = 4
HC = HID + 1


def wait(eng, sem, value):
    if isinstance(value, int) and value <= 0:
        return
    eng.wait_ge(sem, value)


def build(nc, x, ctx_in, pos, Wq, Wkv, Wout, bout, gamma, beta, mu, scale, W1, b1, W2, b2, out):
    ctx = ExitStack()
    with ctx:
        def sb(name, *shape, dt=F32):
            return ctx.enter_context(nc.sbuf_tensor(name, list(shape), dt))

        def split(name, *shape):
            return sb(name + "_h", *shape, dt=F32R), sb(name + "_l", *shape, dt=F32R)

        def sem(name):
            return ctx.enter_context(nc.semaphore(name))

        ident = sb("ident", P, P)
        ones = sb("ones", P, P)
        wqkv = split("wqkv", P, KD + 2, DIM)
        wo = sb("wo", P, KD, DIM)
        mu_raw = sb("mu_raw", P, KD, ES)
        mun = split("mun", P, KD, ES)
        w12_raw = sb("w12_raw", P, 2, ES)
        w1 = split("w1", P, KD, EXPERTS * HID)
        w2 = split("w2", P, EXPERTS // 2, DIM)
        mu_r = sb("mu_r", P, 5, EXPERTS)
        b2s = sb("b2s", EXPERTS, DIM)
        boutb = sb("boutb", P, DIM)
        scaleb = sb("scaleb", P, 1)
        nshift = sb("nshift", P, 1)
        posb = sb("posb", P, TILES, 2)
        ang = sb("ang", P, 2, TILES, 2, 2)
        turns = sb("turns", P, 2, TILES, 2, 2)
        cosb = sb("cosb", P, TILES, 8)
        sinb = sb("sinb", P, TILES, 8)
        mhalf = sb("mhalf", P, TILES)
        threehalf = sb("threehalf", P, TILES)
        hmask = sb("hmask", P, 4)
        hmask_g = sb("hmask_g", P, 16)
        hone = sb("hone", P, 2, 32)

        xa = sb("xa", P, TILES, DIM)
        ctile = sb("ctile", P, 2, CDIM)
        st1 = sb("st1", P, TILES, 6)
        ln1 = sb("ln1", P, 8, TILES)
        xc = sb("xc", P, 2, DIM)
        xn = sb("xn", P, 2, DIM)
        xT = split("xT", P, 3, P)
        ra = sb("ra", P, 64, 8)
        rb = sb("rb", P, 64, 8)
        qkr = sb("qkr", P, 2, DIM)
        qT = sb("qT", P, 2, P)
        kT = sb("kT", P, 2, 4, P)
        vb = sb("vb", P, 2, 2, 2, 272)
        mx = sb("mx", P, GROUPS, 8)
        pb = sb("pb", P, 2, GROUPS, 8, SEQ)
        pT = sb("pT", P, 16, P)
        rc = sb("rc", P, DIM)
        oT = sb("oT", P, DIM)
        st2 = sb("st2", P, TILES, 6)
        ln2 = sb("ln2", P, 8, TILES)
        ss = sb("ss", P, 2)
        sm2 = sb("sm2", P, 2, 8)
        rn = sb("rn", P, 2)
        xlT = split("xlT", P, KD, P)
        eb = sb("eb", P, EXPERTS, SLOTS)
        es = sb("es", P, EXPERTS)
        rs = sb("rs", P, 2, 2)
        rh = sb("rh", P, EXPERTS, 2)
        gT = split("gT", P, EXPERTS // 2, P)
        esT = sb("esT", EXPERTS, P)

        bank = [ctx.enter_context(nc.psum_tensor(f"bank{i}", [P, BANK], F32)) for i in range(8)]

        x_loaded = [sem("x_loaded0"), sem("x_loaded1")]
        wqkv_loaded = sem("wqkv_loaded")
        small_loaded = sem("small_loaded")
        wo_loaded = sem("wo_loaded")
        pos_loaded = sem("pos_loaded")
        mu_loaded = sem("mu_loaded")
        w12_loaded = sem("w12_loaded")
        wb_loaded = sem("wb_loaded")
        ctx_loaded = [sem("ctx_loaded0"), sem("ctx_loaded1")]
        ident_step = sem("ident_step")
        consts_pool = sem("consts_pool")
        consts_dve = sem("consts_dve")
        ang_step = sem("ang_step")
        ang_ready = sem("ang_ready")
        sin_ready = sem("sin_ready")
        rope_ready = sem("rope_ready")
        musq_ready = sem("musq_ready")
        muss_ready = sem("muss_ready")
        muss_clamped = sem("muss_clamped")
        mur_step = sem("mur_step")
        mur_ready = sem("mur_ready")
        diag_ready = sem("diag_ready")
        rb_filled = sem("rb_filled")
        rb_ready = sem("rb_ready")
        muscale_step = sem("muscale_step")
        split_step = sem("split_step")
        w12_ready = sem("w12_ready")
        mu_ready = sem("mu_ready")
        wqkv_step = sem("wqkv_step")
        wqkv_ready = sem("wqkv_ready")
        shift_step = sem("shift_step")
        shift_ready = sem("shift_ready")
        st1_ready = sem("st1_ready")
        var1_step = sem("var1_step")
        var1_ready = sem("var1_ready")
        r1_step = sem("r1_step")
        r1_ready = sem("r1_ready")
        xc_done = sem("xc_done")
        xn_ready = sem("xn_ready")
        xb_ready = sem("xb_ready")
        xT_filled = sem("xT_filled")
        xT_split = sem("xT_split")
        xT_ready = sem("xT_ready")
        qk_filled = sem("qk_filled")
        v_filled = sem("v_filled")
        ropeab_done = sem("ropeab_done")
        qk_roped = sem("qk_roped")
        v_ready = sem("v_ready")
        kq_filled = sem("kq_filled")
        q_ready = sem("q_ready")
        k0_ready = sem("k0_ready")
        k1_ready = sem("k1_ready")
        hmask_step = sem("hmask_step")
        s_filled = sem("s_filled")
        max_done = sem("max_done")
        sub_done = sem("sub_done")
        p_ready = sem("p_ready")
        pT_filled = sem("pT_filled")
        pT_ready = sem("pT_ready")
        o_filled = sem("o_filled")
        rc_done = sem("rc_done")
        oT_ready = sem("oT_ready")
        a_filled = sem("a_filled")
        x1_ready = sem("x1_ready")
        st2_ready = sem("st2_ready")
        var_step = sem("var_step")
        var_ready = sem("var_ready")
        r2_step = sem("r2_step")
        r2_ready = sem("r2_ready")
        z_ready = sem("z_ready")
        aff_step = sem("aff_step")
        xl_ready = sem("xl_ready")
        ss_ready = sem("ss_ready")
        ss_clamped = sem("ss_clamped")
        rn_step = sem("rn_step")
        rn_ready = sem("rn_ready")
        xlT_filled = sem("xlT_filled")
        xlT_split = sem("xlT_split")
        xlT_ready = sem("xlT_ready")
        l_filled = sem("l_filled")
        e_ready = sem("e_ready")
        xw_step = sem("xw_step")
        xw_const = sem("xw_const")
        xw_filled = sem("xw_filled")
        xw_ready = sem("xw_ready")
        eT_filled = sem("eT_filled")
        eT_act = sem("eT_act")
        eT_dve = sem("eT_dve")
        es_ready = sem("es_ready")
        h_filled = sem("h_filled")
        rh_done = sem("rh_done")
        hn_ready = sem("hn_ready")
        h_ready = sem("h_ready")
        g_filled = sem("g_filled")
        gT_split = sem("gT_split")
        gT_ready = sem("gT_ready")
        esT_filled = sem("esT_filled")
        esT_ready = sem("esT_ready")
        rs_step = sem("rs_step")
        y_filled = sem("y_filled")
        yo_ready = sem("yo_ready")
        stored = [sem("stored0"), sem("stored1")]

        x_d = x.rearrange("b s d -> (b s) d").rearrange("(t p) d -> p t d", p=P)
        ctx_d = ctx_in.rearrange("b s d -> (b s) d").rearrange("(t p) d -> p t d", p=P)
        pos_d = pos.rearrange("b s c -> (b s) c").rearrange("(t p) c -> p t c", p=P)
        out_d = out.rearrange("b s d -> (b s) d").rearrange("(t p) d -> p t d", p=P)

        def row(v, n):
            return v.rearrange("(a d) -> a d", a=1).broadcast_to([P, n])

        PER = BANK // (2 * HC)
        HG = [range(i, min(i + PER, EXPERTS)) for i in range(0, EXPERTS, PER)]
        GG = [(HG[i][0], HG[min(i + 1, len(HG) - 1)][-1] + 1) for i in range(0, len(HG), 2)]
        NB = (6, 7, 5, 6)
        LB = (0, 1, 2, 5)
        HB = (4, 5, 3)

        def flat(t):
            return t[:].rearrange("p a b -> p (a b)")

        wqkv_raw = flat(pT)[:, 0:(KD + 2) * DIM].rearrange("p (k n) -> p k n", n=DIM)
        w1_raw, w2_raw = w12_raw[:, 0, :], w12_raw[:, 1, :]
        musq = [flat(eb), w12_raw[:, 0, :]]
        diag = w12_raw[:, 1, :].rearrange("p (e s) -> p e s", s=P)
        mu_rb = flat(eb)
        eT = mu_raw[:, 0, :].rearrange("p (e s) -> p e s", s=P)
        b1b = mu_raw[:, 1, 0:EXPERTS * HID].rearrange("p (e h) -> p e h", h=HID)
        gammab = mu_raw[:, 1, 1024:1024 + DIM]
        betab = mu_raw[:, 1, 1024 + DIM:1024 + 2 * DIM]
        w12f = flat(w12_raw)
        XW = EXPERTS * 2 * HC
        xw = w12f[:, 0:XW].rearrange("p (e c) -> p e c", c=2 * HC)
        yo = w12f[:, XW:XW + 2 * DIM].rearrange("p (a d) -> p a d", d=DIM)
        sq = w12f[:, XW + 2 * DIM:XW + 3 * DIM]
        hb = pb[:, 1].rearrange("p g h k -> p (g h k)").rearrange("p (e b h) -> p e b h", b=2, h=HID)
        xl = xc

        block = ctx.enter_context(nc.Block())

        @block.sync
        def _(sp):
            def load_ctx(t, p):
                wait(sp, xT_filled, t - 1)
                sp.dma_start(ctile[:, p, :], ctx_d[:, t, :]).then_inc(ctx_loaded[p], 16)

            def store(t, p):
                sp.wait_ge(yo_ready, t + 1)
                sp.dma_start(out_d[:, t, :], yo[:, p, :]).then_inc(stored[p], 16)

            sp.dma_start(xa[:, 0:AHEAD, :], x_d[:, 0:AHEAD, :]).then_inc(x_loaded[0], 16)
            load_ctx(0, 0)
            sp.dma_start(wqkv_raw[:, 0:KD, :], Wq.rearrange("(k p) n -> p k n", p=P)).then_inc(wqkv_loaded, 16)
            sp.dma_start(wqkv_raw[:, KD:KD + 2, :], Wkv.rearrange("p (k n) -> p k n", k=2)).then_inc(wqkv_loaded, 16)
            sp.dma_start(posb[:], pos_d).then_inc(pos_loaded, 16)
            sp.dma_start(boutb[:], row(bout, DIM)).then_inc(small_loaded, 16)
            sp.dma_start(scaleb[:], row(scale, 1)).then_inc(small_loaded, 16)
            load_ctx(1, 1)
            sp.dma_start(xa[:, AHEAD:TILES, :], x_d[:, AHEAD:TILES, :]).then_inc(x_loaded[1], 16)
            sp.dma_start(wo[:], Wout.rearrange("(k p) n -> p k n", p=P)).then_inc(wo_loaded, 16)
            sp.dma_start(mu_raw[:], mu.rearrange("(k p) e s -> p k (e s)", p=P)).then_inc(mu_loaded, 16)
            with sp.Fori(1, 5) as i:
                for p in range(2):
                    load_ctx(i * 2 + p, p)
            sp.wait_ge(rb_filled, 4)
            for k in range(KD):
                sp.dma_start(w1_raw[:, k * 1024:(k + 1) * 1024].rearrange("p (e h) -> p e h", h=HID),
                             W1[:, k * P:(k + 1) * P, :].rearrange("e p h -> p e h")).then_inc(w12_loaded, 16)
            sp.dma_start(w2_raw.rearrange("p (k d) -> p k d", d=DIM),
                         W2.rearrange("e h d -> (e h) d").rearrange("(k p) d -> p k d", p=P)).then_inc(w12_loaded, 16)
            with sp.Fori(5, TILES // 2) as i:
                for p in range(2):
                    load_ctx(i * 2 + p, p)
            sp.wait_ge(mu_ready, 2)
            sp.dma_start(b1b.rearrange("p e h -> p (e h)"), row(b1.rearrange("e h -> (e h)"), EXPERTS * HID))\
                .then_inc(wb_loaded, 16)
            sp.dma_start(b2s[:], b2).then_inc(wb_loaded, 16)
            sp.dma_start(gammab, row(gamma, DIM)).then_inc(wb_loaded, 16)
            sp.dma_start(betab, row(beta, DIM)).then_inc(wb_loaded, 16)
            with sp.Fori(0, TILES // 2) as i:
                for p in range(2):
                    store(i * 2 + p, p)
            for p in range(2):
                sp.wait_ge(stored[p], 16 * TILES // 2)

        @block.gpsimd
        def _(pool):
            g = nc.gpsimd
            g.memset(ident[:], 0.0).then_inc(ident_step, 1)
            pool.wait_ge(ident_step, 1)
            g.affine_select(out=ident[:], in_=ident[:], compare_op=ALU.not_equal, fill=1.0, base=0,
                            pattern=[[-1, P]], channel_multiplier=1).then_inc(consts_pool, 1)
            g.memset(mhalf[:], -0.5).then_inc(consts_pool, 1)
            g.memset(ones[:], 1.0).then_inc(consts_pool, 1)
            g.memset(threehalf[:], 1.5).then_inc(consts_pool, 1)
            pool.wait_ge(consts_pool, 4)

            def rsqrt(a, r, tmp, step, base):
                n = r.shape[1]
                g.tensor_tensor(tmp[0], a, mhalf[:, 0:n], ALU.pow).then_inc(step, 1)
                g.tensor_tensor(tmp[2], a, mhalf[:, 0:n], ALU.mult).then_inc(step, 1)
                pool.wait_ge(step, base + 1)
                g.tensor_tensor(tmp[1], tmp[0], tmp[0], ALU.mult).then_inc(step, 1)
                pool.wait_ge(step, base + 3)
                g.tensor_tensor(tmp[1], tmp[1], tmp[2], ALU.mult).then_inc(step, 1)
                pool.wait_ge(step, base + 4)
                g.tensor_tensor(tmp[1], tmp[1], threehalf[:, 0:n], ALU.add).then_inc(step, 1)
                pool.wait_ge(step, base + 5)
                return g.tensor_tensor(r, tmp[0], tmp[1], ALU.mult)

            def norm_x(t, p):
                g.tensor_tensor(xc[:, p, :], xa[:, t, :], ln1[:, 4, t].unsqueeze(1).broadcast_to([P, DIM]),
                                ALU.subtract).then_inc(xc_done, 1)
                pool.wait_ge(xc_done, t + 1)
                wait(pool, xT_filled, t - 1)
                g.tensor_tensor(xn[:, p, :], xc[:, p, :], ln1[:, 6, t].unsqueeze(1).broadcast_to([P, DIM]),
                                ALU.mult).then_inc(xn_ready, 1)
                g.tensor_tensor(xa[:, t, :], xa[:, t, :], boutb[:], ALU.add).then_inc(xb_ready, 1)

            def deviations(L, t0, t1, step, base, done):
                rsqrt(L[:, 5, t0:t1], L[:, 6, t0:t1], (L[:, 1, t0:t1], L[:, 3, t0:t1], L[:, 7, t0:t1]), step, base)\
                    .then_inc(done, 1)

            def split_pool(raw, halves, base, done):
                high, low = halves
                g.tensor_copy(high, raw).then_inc(split_step, 1)
                pool.wait_ge(split_step, base + 1)
                g.tensor_tensor(low, raw, high.bitcast(F32), ALU.subtract).then_inc(done, 1)

            pool.wait_ge(var1_ready, 1)
            deviations(ln1, 0, AHEAD, r1_step, 0, r1_ready)
            pool.wait_ge(small_loaded, 32)
            pool.wait_ge(r1_ready, 1)
            for t in range(AHEAD):
                norm_x(t, t % 2)
            pool.wait_ge(var1_ready, 2)
            deviations(ln1, AHEAD, TILES, r1_step, 5, r1_ready)
            pool.wait_ge(r1_ready, 2)
            pool.wait_ge(mu_loaded, 16)
            for k in range(KD):
                g.tensor_tensor(musq[k], mu_raw[:, k, :], mu_raw[:, k, :], ALU.mult).then_inc(musq_ready, 1)
            pool.wait_ge(musq_ready, 2)
            g.tensor_tensor(musq[0], musq[0], musq[1], ALU.add).then_inc(musq_ready, 1)
            with pool.Fori(2, 5) as i:
                for p in range(2):
                    norm_x(i * 2 + p, p)
            pool.wait_ge(muss_clamped, 1)
            R = [mu_r[:, i, :] for i in range(5)]
            rsqrt(R[0], R[1], (R[2], R[3], R[4]), mur_step, 0).then_inc(mur_ready, 1)
            pool.wait_ge(mur_ready, 1)
            g.tensor_tensor(diag, ident[:].unsqueeze(1).broadcast_to([P, EXPERTS, P]),
                            R[1].unsqueeze(2).broadcast_to([P, EXPERTS, P]), ALU.mult).then_inc(diag_ready, 1)
            pool.wait_ge(rb_ready, 4)
            for k in range(KD):
                with pool.Fori(5 + k, 6 + k) as i:
                    for p in range(2):
                        norm_x(i * 2 + p, p)
                g.tensor_tensor(mu_raw[:, k, :], mu_raw[:, k, :], mu_rb, ALU.mult).then_inc(muscale_step, 1)
                pool.wait_ge(muscale_step, k + 1)
                split_pool(mu_raw[:, k, :], [h[:, k, :] for h in mun], k, mu_ready)
            with pool.Fori(7, TILES // 2) as i:
                for p in range(2):
                    norm_x(i * 2 + p, p)
            pool.wait_ge(w12_loaded, 48)
            split_pool(w1_raw, [flat(h) for h in w1], 2, w12_ready)
            split_pool(w2_raw, [flat(h) for h in w2], 3, w12_ready)
            pool.wait_ge(w12_ready, 2)
            g.memset(w12f[:, 0:XW], 0.0).then_inc(xw_step, 1)
            pool.wait_ge(xw_step, 1)
            for b in range(2):
                g.memset(xw[64 * b:64 * b + 64, :, b * HC + HID:b * HC + HC], 1.0).then_inc(xw_const, 1)
            pool.wait_ge(xw_const, 2)

            pool.wait_ge(var_ready, 1)
            deviations(ln2, 0, TILES - 4, r2_step, 0, r2_ready)

            def affine(t, p):
                pool.wait_ge(z_ready, t + 1)
                g.tensor_tensor(xl[:, p, :], xl[:, p, :], gammab, ALU.mult).then_inc(aff_step, 1)
                pool.wait_ge(aff_step, t + 1)
                g.tensor_tensor(xl[:, p, :], xl[:, p, :], betab, ALU.add).then_inc(xl_ready, 1)

            def row_scale(t, p):
                s = sm2[:, p, :]
                pool.wait_ge(ss_clamped, t + 1)
                rsqrt(s[:, 0:1], s[:, 3:4], (s[:, 1:2], s[:, 2:3], s[:, 4:5]), rn_step, t * 6).then_inc(rn_step, 1)
                pool.wait_ge(rn_step, t * 6 + 6)
                wait(pool, e_ready, (t - 1) * 4)
                g.tensor_tensor(rn[:, p:p + 1], s[:, 3:4], scaleb[:], ALU.mult).then_inc(rn_ready, 1)

            pool.wait_ge(wb_loaded, 64)
            affine(0, 0)
            row_scale(0, 0)
            affine(1, 1)
            for t in range(2):
                row_scale(t + 1, 1 - t)
                affine(t + 2, t)
                if t == 0:
                    pool.wait_ge(var_ready, 2)
                    deviations(ln2, TILES - 4, TILES, r2_step, 5, r2_ready)
            with pool.Fori(1, TILES // 2 - 1) as i:
                for p in range(2):
                    row_scale(i * 2 + p + 1, 1 - p)
                    affine(i * 2 + p + 2, p)
            row_scale(TILES - 1, 1)

        @block.scalar
        def _(act):
            a = nc.scalar
            act.wait_ge(ang_ready, 1)
            a.activation(ang[:], ang[:], ACT.Sin).then_inc(sin_ready, 1)
            act.wait_ge(wqkv_loaded, 32)
            a.copy(flat(wqkv[0]), flat(wqkv_raw)).then_inc(wqkv_step, 1)

            def exp_group(t, p, gr):
                act.wait_ge(sub_done, t * 4 + gr + 1)
                a.activation(pb[:, p, gr], pb[:, p, gr], ACT.Exp, scale=HD ** -0.5).then_inc(p_ready, 1)

            def pT_copy(t, gr):
                act.wait_ge(pT_filled, t * 4 + gr + 1)
                a.copy(pT[:, 4 * gr:4 * gr + 4, :].rearrange("p a b -> p (a b)"), bank[6 + gr % 2][:])\
                    .then_inc(pT_ready, 1)

            def v_copy(t, p):
                act.wait_ge(v_filled, t + 1)
                wait(act, o_filled, t - 1)
                for b in range(2):
                    for j in range(2):
                        src = bank[6][64 * b:64 * b + 64, 0:DIM].rearrange(
                            "p (m r j d) -> p r m j d", m=8, r=2, j=2)[:, :, :, j, :]
                        dst = vb[64 * j:64 * j + 64, p, b, :, 0:256].rearrange(
                            "p r (m c) -> p r m c", c=32)[:, :, :, 8 * j:8 * j + 8]
                        a.copy(dst, src).then_inc(v_ready, 1)

            def q_copy(t):
                act.wait_ge(kq_filled, t * 2 + 2)
                a.copy(qT[:], bank[3][:, 0:DIM].rearrange("p (j n) -> p j n", j=2)).then_inc(q_ready, 1)

            def k1_copy(t):
                for j in range(4):
                    a.activation(kT[:, 1, j, :], bank[3][:, DIM:DIM + P], ACT.Copy, scale=hmask[:, j:j + 1])\
                        .then_inc(k1_ready, 1)

            def xT_high(t):
                act.wait_ge(xT_filled, t + 1)
                a.copy(flat(xT[0]), bank[7][:, 0:3 * P]).then_inc(xT_split, 1)

            def step(s, p, before=True, after=True, ahead=True):
                for g0 in (0, 2):
                    if before:
                        for gr in (g0, g0 + 1):
                            pT_copy(s - 1, gr)
                    for gr in (g0, g0 + 1):
                        exp_group(s, p, gr)
                if after:
                    v_copy(s + 1, 1 - p)
                    q_copy(s + 1)
                    if ahead:
                        xT_high(s + 2)
                    k1_copy(s + 1)

            act.wait_ge(consts_dve, 4)
            xT_high(0)
            v_copy(0, 0)
            xT_high(1)
            act.wait_ge(hmask_step, 2)
            q_copy(0)
            k1_copy(0)
            step(0, 0, before=False)
            step(1, 1)
            with act.Fori(1, 4) as i:
                for p in range(2):
                    step(i * 2 + p, p)
            for c in range(4):
                act.wait_ge(rb_filled, c + 1)
                a.copy(mu_rb[:, c * BANK:(c + 1) * BANK], bank[NB[c]][:]).then_inc(rb_ready, 1)
            with act.Fori(4, TILES // 2 - 1) as i:
                for p in range(2):
                    step(i * 2 + p, p)
            step(TILES - 2, 0, ahead=False)
            step(TILES - 1, 1, after=False, ahead=False)
            def sumsq(t, p):
                act.wait_ge(xl_ready, t + 1)
                a.activation(sq, xl[:, p, :], ACT.Square, accum_out=ss[:, p:p + 1]).then_inc(ss_ready, 1)

            def slot_exps(t, p):
                act.wait_ge(rn_ready, t + 1)
                wait(act, es_ready, t)
                for c in range(4):
                    act.wait_ge(l_filled, t * 4 + c + 1)
                    a.activation(eb[:, 4 * c:4 * c + 4, :].rearrange("p a b -> p (a b)"), bank[LB[c]][:], ACT.Exp,
                                 scale=rn[:, p:p + 1], bias=nshift[:]).then_inc(e_ready, 1)

            def eT_copy(t, groups):
                for gr in groups:
                    act.wait_ge(eT_filled, t * 4 + gr + 1)
                    a.copy(eT[:, 4 * gr:4 * gr + 4, :].rearrange("p a b -> p (a b)"),
                           bank[(6, 7, 0, 1)[gr]][:]).then_inc(eT_act, 1)

            def gelus(t):
                for i, (e0, e1) in enumerate(GG):
                    act.wait_ge(hn_ready, t * len(HG) + min(2 * i + 2, len(HG)))
                    a.activation(hb[:, e0:e1], hb[:, e0:e1], ACT.Gelu).then_inc(h_ready, 1)

            def gT_high(t):
                for c in range(2):
                    act.wait_ge(g_filled, t * 2 + c + 1)
                    a.copy(gT[0][:, 4 * c:4 * c + 4, :].rearrange("p a b -> p (a b)"), bank[(6, 3)[c]][:])\
                        .then_inc(gT_split, 1)

            def ffn_step(s, p, last=False, sums=True):
                eT_copy(s, range(4) if last else (0, 2))
                gelus(s)
                if not last:
                    slot_exps(s + 1, 1 - p)
                gT_high(s)
                if sums:
                    sumsq(s + 2, p)

            act.wait_ge(shift_ready, 1)
            act.wait_ge(w12_ready, 2)
            sumsq(0, 0)
            for gr in range(2):
                pT_copy(TILES - 1, gr)
            slot_exps(0, 0)
            for gr in range(2, 4):
                pT_copy(TILES - 1, gr)
            sumsq(1, 1)
            with act.Fori(0, TILES // 2 - 1) as i:
                for p in range(2):
                    ffn_step(i * 2 + p, p)
            ffn_step(TILES - 2, 0, sums=False)
            ffn_step(TILES - 1, 1, last=True, sums=False)

        @block.vector
        def _(dve):
            v = nc.vector
            v.memset(vb[:].rearrange("p a b c d -> p (a b c d)"), 0.0).then_inc(consts_dve, 1)
            v.memset(hone[:].rearrange("p a b -> p (a b)"), 0.0).then_inc(consts_dve, 1)
            dve.wait_ge(consts_dve, 2)
            for b in range(2):
                hv = hone[64 * b:64 * b + 64].rearrange("p r (q j d) -> p r q j d", q=2, j=2)
                for r in range(2):
                    m = v.memset(hv[:, r, r, b, :], 1.0)
                m.then_inc(consts_dve, 1)

            def moments(st, L, t0, t1, var_scale, var_bias, step, base, done):
                L = [L[:, i, t0:t1] for i in range(8)]
                st = [st[:, t0:t1, i] for i in range(6)]
                v.tensor_tensor(L[0], st[1], st[4], ALU.add).then_inc(step, 1)
                v.tensor_tensor(L[1], st[1], st[4], ALU.subtract).then_inc(step, 1)
                v.tensor_tensor(L[2], st[2], st[5], ALU.add).then_inc(step, 1)
                dve.wait_ge(step, base + 3)
                v.tensor_scalar(L[4], L[0], 0.5, None, ALU.mult).then_inc(step, 1)
                v.tensor_tensor(L[3], L[1], L[1], ALU.mult).then_inc(step, 1)
                dve.wait_ge(step, base + 5)
                v.tensor_scalar(L[3], L[3], DIM / 4.0, None, ALU.mult).then_inc(step, 1)
                dve.wait_ge(step, base + 6)
                v.tensor_tensor(L[2], L[2], L[3], ALU.add).then_inc(step, 1)
                dve.wait_ge(step, base + 7)
                v.tensor_scalar(L[5], L[2], var_scale / DIM, var_bias, ALU.mult, ALU.add).then_inc(done, 1)

            dve.wait_ge(x_loaded[0], 16)
            for t in range(AHEAD):
                v.bn_stats(st1[:, t, :], xa[:, t, :]).then_inc(st1_ready, 1)
            dve.wait_ge(st1_ready, AHEAD)
            moments(st1, ln1, 0, AHEAD, 1.0, LN_EPS, var1_step, 0, var1_ready)

            PI = 3.141592653589793
            PI32 = 3.1415925
            TURN_HI, ROUND = 6.28125, 12582912.0
            TURN_LO = 2 * PI - TURN_HI
            dve.wait_ge(pos_loaded, 16)
            for f in range(2):
                v.tensor_scalar(ang[:, 1, :, :, f], posb[:], ROPE_FREQ[f], None, ALU.mult).then_inc(ang_step, 1)
            dve.wait_ge(ang_step, 2)
            v.tensor_scalar(ang[:, 0], ang[:, 1], PI / 2, None, ALU.add).then_inc(ang_step, 1)
            dve.wait_ge(ang_step, 3)
            v.tensor_scalar(turns[:], ang[:], 1 / (2 * PI), ROUND, ALU.mult, ALU.add).then_inc(ang_step, 1)
            dve.wait_ge(ang_step, 4)
            v.tensor_scalar(turns[:], turns[:], ROUND, None, ALU.subtract).then_inc(ang_step, 1)
            dve.wait_ge(ang_step, 5)
            af, tf = (z[:].rearrange("p a t c f -> p (a t c f)") for z in (ang, turns))
            v.scalar_tensor_tensor(out=af, in0=tf, scalar=-TURN_HI, in1=af, op0=ALU.mult, op1=ALU.add)\
                .then_inc(ang_step, 1)
            dve.wait_ge(ang_step, 6)
            v.scalar_tensor_tensor(out=af, in0=tf, scalar=-TURN_LO, in1=af, op0=ALU.mult, op1=ALU.add)\
                .then_inc(ang_step, 1)
            dve.wait_ge(ang_step, 7)
            v.tensor_scalar(af, af, PI32, -PI32, ALU.min, ALU.max).then_inc(ang_ready, 1)

            def xT_low(t):
                dve.wait_ge(xT_split, t + 1)
                v.tensor_tensor(flat(xT[1]), bank[7][:, 0:3 * P], flat(xT[0]).bitcast(F32), ALU.subtract)\
                    .then_inc(xT_ready, 1)

            def rope_products(t):
                dve.wait_ge(qk_filled, t + 1)
                src = bank[4][:].rearrange("p (h c) -> p h c", c=8)
                v.tensor_tensor(ra[:], src, cosb[:, t, :].unsqueeze(1).broadcast_to([P, 64, 8]), ALU.mult)\
                    .then_inc(ropeab_done, 1)
                v.tensor_tensor(rb[:], src, sinb[:, t, :].unsqueeze(1).broadcast_to([P, 64, 8]), ALU.mult)\
                    .then_inc(ropeab_done, 1)

            def rope_sums(t):
                wait(dve, kq_filled, t * 2)
                dve.wait_ge(ropeab_done, t * 2 + 2)
                for e in range(2):
                    v.tensor_tensor(qkr[:].rearrange("p a (n e) -> p (a n) e", e=2)[:, :, e],
                                    ra[:].rearrange("p h (c e) -> p (h c) e", e=2)[:, :, e],
                                    rb[:].rearrange("p h (c e) -> p (h c) e", e=2)[:, :, 1 - e],
                                    ALU.add).then_inc(qk_roped, 1)

            def k0_copy(t):
                dve.wait_ge(kq_filled, t * 2 + 1)
                v.tensor_tensor(kT[:, 0], bank[2][:, 0:P].unsqueeze(1).broadcast_to([P, 4, P]),
                                hmask[:].unsqueeze(2).broadcast_to([P, 4, P]), ALU.mult).then_inc(k0_ready, 1)

            def softmax_max(t, gr):
                dve.wait_ge(s_filled, t * 4 + gr + 1)
                v.reduce_max(mx[:, gr, :], bank[gr][:].rearrange("p (h k) -> p h k", k=SEQ), AX.X)\
                    .then_inc(max_done, 1)

            def softmax_sub(t, p, gr):
                dve.wait_ge(max_done, t * 4 + gr + 1)
                v.tensor_tensor(pb[:, p, gr], bank[gr][:].rearrange("p (h k) -> p h k", k=SEQ),
                                mx[:, gr, :].unsqueeze(2).broadcast_to([P, 8, SEQ]), ALU.subtract)\
                    .then_inc(sub_done, 1)

            def softmax(t, p, g0):
                for gr in (g0, g0 + 1):
                    softmax_max(t, gr)
                for gr in (g0, g0 + 1):
                    softmax_sub(t, p, gr)

            def normalise(t):
                dve.wait_ge(o_filled, t + 1)
                v.reciprocal(rc[:], bank[4][:, DIM:2 * DIM]).then_inc(rc_done, 1)
                dve.wait_ge(rc_done, t + 1)
                v.tensor_tensor(oT[:], bank[4][:, 0:DIM], rc[:], ALU.mult).then_inc(oT_ready, 1)

            def residual(t, b=5):
                dve.wait_ge(a_filled, t + 1)
                dve.wait_ge(xb_ready, t + 1)
                v.tensor_tensor(xa[:, t, :], bank[b][:, 0:DIM], xa[:, t, :], ALU.add).then_inc(x1_ready, 1)
                dve.wait_ge(x1_ready, t + 1)
                v.bn_stats(st2[:, t, :], xa[:, t, :]).then_inc(st2_ready, 1)

            def step(s, p, before=True, after=True, out=True, ahead=True, norms=False):
                softmax(s, p, 0)
                if after:
                    rope_products(s + 1)
                if norms:
                    dve.wait_ge(muss_ready, 1)
                    v.tensor_scalar(mu_r[:, 0, :], bank[5][:, DIM:DIM + EXPERTS], L2_EPS * L2_EPS, None, ALU.max)\
                        .then_inc(muss_clamped, 1)
                softmax(s, p, 2)
                if after:
                    rope_sums(s + 1)
                if out:
                    residual(s - 2)
                if after:
                    k0_copy(s + 1)
                if ahead:
                    xT_low(s + 2)
                if before:
                    normalise(s - 1)

            dve.wait_ge(wqkv_step, 1)
            v.tensor_tensor(flat(wqkv[1]), flat(wqkv_raw), flat(wqkv[0]).bitcast(F32), ALU.subtract)\
                .then_inc(wqkv_ready, 1)
            xT_low(0)
            dve.wait_ge(sin_ready, 1)
            for e in range(2):
                dst = cosb[:].rearrange("p t (c f e) -> p t c f e", c=2, f=2)[:, :, :, :, e]
                v.tensor_copy(dst.rearrange("p t c f -> p (t c) f"), ang[:, 0].rearrange("p t c f -> p (t c) f"))\
                    .then_inc(rope_ready, 1)
                dst = sinb[:].rearrange("p t (c f e) -> p t c f e", c=2, f=2)[:, :, :, :, e]
                v.tensor_scalar(dst.rearrange("p t c f -> p (t c) f"), ang[:, 1].rearrange("p t c f -> p (t c) f"),
                                1.0 - 2.0 * e, None, ALU.mult).then_inc(rope_ready, 1)
            dve.wait_ge(rope_ready, 4)
            rope_products(0)
            xT_low(1)
            rope_sums(0)
            dve.wait_ge(consts_pool, 4)
            v.reduce_sum(hmask_g[:], ident[:].rearrange("p (n d) -> p n d", d=HD), AX.X).then_inc(hmask_step, 1)
            dve.wait_ge(hmask_step, 1)
            v.reduce_sum(hmask[:], hmask_g[:].rearrange("p (g j) -> p j g", j=4), AX.X).then_inc(hmask_step, 1)
            dve.wait_ge(hmask_step, 2)
            k0_copy(0)
            dve.wait_ge(x_loaded[1], 16)
            for t in range(AHEAD, AHEAD + 4):
                v.bn_stats(st1[:, t, :], xa[:, t, :]).then_inc(st1_ready, 1)
            rope_products(1)
            rope_sums(1)
            dve.wait_ge(small_loaded, 32)
            v.tensor_scalar(nshift[:], scaleb[:], -1.0, None, ALU.mult).then_inc(shift_step, 1)
            dve.wait_ge(shift_step, 1)
            v.tensor_tensor(nshift[:], nshift[:], scaleb[:], ALU.min).then_inc(shift_step, 1)
            dve.wait_ge(shift_step, 2)
            v.tensor_scalar(nshift[:], nshift[:], SAFE, 0.0, ALU.add, ALU.min).then_inc(shift_ready, 1)

            softmax(0, 0, 0)
            softmax(0, 0, 2)
            k0_copy(1)
            xT_low(2)
            with dve.Fori(AHEAD // 4 + 1, TILES // 4) as i:
                for u in range(4):
                    v.bn_stats(st1[:, i * 4 + u, :], xa[:, i * 4 + u, :]).then_inc(st1_ready, 1)
            dve.wait_ge(st1_ready, TILES)
            moments(st1, ln1, AHEAD, TILES, 1.0, LN_EPS, var1_step, 7, var1_ready)
            step(1, 1, out=False)
            with dve.Fori(1, 3) as i:
                for p in range(2):
                    step(i * 2 + p, p)
            step(6, 0, norms=True)
            step(7, 1)
            with dve.Fori(4, TILES // 2 - 1) as i:
                for p in range(2):
                    step(i * 2 + p, p)
            dve.wait_ge(st2_ready, TILES - 4)
            moments(st2, ln2, 0, TILES - 4, 1 + LN_EPS, LN_EPS * LN_EPS, var_step, 0, var_ready)
            step(TILES - 2, 0, ahead=False)

            def center(t, p):
                wait(dve, xlT_filled, t - 1)
                v.tensor_scalar(xl[:, p, :], xa[:, t, :], ln2[:, 4, t].unsqueeze(1), ln2[:, 6, t].unsqueeze(1),
                                ALU.subtract, ALU.mult).then_inc(z_ready, 1)

            def clamp(t, p):
                dve.wait_ge(ss_ready, t + 1)
                wait(dve, rn_ready, t - 1)
                v.tensor_scalar(sm2[:, p, 0:1], ss[:, p:p + 1], L2_EPS * L2_EPS, None, ALU.max)\
                    .then_inc(ss_clamped, 1)

            def xlT_copy(t):
                dve.wait_ge(xlT_filled, t + 1)
                v.tensor_copy(flat(xlT[0]), bank[2][:, 0:DIM]).then_inc(xlT_split, 1)
                dve.wait_ge(xlT_split, t + 1)
                v.tensor_tensor(flat(xlT[1]), bank[2][:, 0:DIM], flat(xlT[0]).bitcast(F32), ALU.subtract)\
                    .then_inc(xlT_ready, 1)

            def xw_copy(t):
                for c in range(2):
                    dve.wait_ge(xw_filled, t * 2 + c + 1)
                    for b in range(2):
                        rows = slice(64 * b, 64 * b + 64)
                        v.tensor_tensor(xw[rows, 8 * c:8 * c + 8, b * HC:b * HC + HID],
                                        bank[2 + c][rows].rearrange("p (e h) -> p e h", h=HID),
                                        b1b[rows, 8 * c:8 * c + 8, :], ALU.add).then_inc(xw_ready, 1)

            def eT_copy(t, gr):
                dve.wait_ge(eT_filled, t * 4 + gr + 1)
                v.tensor_copy(eT[:, 4 * gr:4 * gr + 4, :].rearrange("p a b -> p (a b)"), bank[(6, 7, 0, 1)[gr]][:])\
                    .then_inc(eT_dve, 1)

            def sums(t, p):
                wait(dve, esT_filled, t)
                dve.wait_ge(e_ready, t * 4 + 4)
                v.reduce_sum(es[:], eb[:], AX.X).then_inc(es_ready, 1)
                dve.wait_ge(es_ready, t + 1)
                v.reduce_sum(rs[:, p, 0:1], es[:], AX.X).then_inc(rs_step, 1)
                dve.wait_ge(rs_step, t * 2 + 1)
                v.reciprocal(rs[:, p, 1:2], rs[:, p, 0:1]).then_inc(rs_step, 1)

            def hidden(t, last):
                for i, gr in enumerate(HG):
                    if i == 3 and not last:
                        eT_copy(t, 3)
                    n, e0 = len(gr), gr[0]
                    dve.wait_ge(h_filled, t * len(HG) + i + 1)
                    src = bank[HB[i % 3]][:, 0:n * 2 * HC].rearrange("p (n b c) -> p n b c", b=2, c=HC)
                    v.reciprocal(rh[:, e0:e0 + n, :], src[:, :, :, HID]).then_inc(rh_done, 1)
                    dve.wait_ge(rh_done, t * len(HG) + i + 1)
                    v.tensor_tensor(hb[:, e0:e0 + n], src[:, :, :, 0:HID],
                                    rh[:, e0:e0 + n, :].unsqueeze(3).broadcast_to([P, n, 2, HID]),
                                    ALU.mult).then_inc(hn_ready, 1)

            def gT_low(t):
                dve.wait_ge(esT_filled, t + 1)
                v.tensor_copy(esT[:], bank[7][0:EXPERTS, 0:P]).then_inc(esT_ready, 1)
                for c in range(2):
                    high, low = (h[:, 4 * c:4 * c + 4, :].rearrange("p a b -> p (a b)") for h in gT)
                    dve.wait_ge(gT_split, t * 2 + c + 1)
                    v.tensor_tensor(low, bank[(6, 3)[c]][:], high.bitcast(F32), ALU.subtract).then_inc(gT_ready, 1)

            def finish(t, p):
                dve.wait_ge(y_filled, t + 1)
                dve.wait_ge(rs_step, t * 2 + 2)
                if not isinstance(t, int) or t >= 2:
                    dve.wait_ge(stored[p], (t - p) * 8)
                v.scalar_tensor_tensor(out=yo[:, p, :], in0=bank[4][:, 0:DIM], scalar=rs[:, p, 1:2], in1=xa[:, t, :],
                                       op0=ALU.mult, op1=ALU.add).then_inc(yo_ready, 1)

            def ffn_step(s, p, last=False, ahead=True):
                if not last:
                    clamp(s + 1, 1 - p)
                xw_copy(s)
                if not last:
                    xlT_copy(s + 1)
                hidden(s, last)
                if not last:
                    eT_copy(s, 1)
                if ahead:
                    center(s + 2, p)
                gT_low(s)
                if not last:
                    sums(s + 1, 1 - p)
                finish(s, p)

            dve.wait_ge(r2_ready, 1)
            center(0, 0)
            center(1, 1)
            softmax(TILES - 1, 1, 0)
            softmax(TILES - 1, 1, 2)
            residual(TILES - 3)
            xlT_copy(0)
            clamp(0, 0)
            normalise(TILES - 2)
            residual(TILES - 2, 3)
            dve.wait_ge(wb_loaded, 64)
            dve.wait_ge(xw_const, 2)
            sums(0, 0)
            normalise(TILES - 1)
            residual(TILES - 1)
            ffn_step(0, 0)
            dve.wait_ge(st2_ready, TILES)
            moments(st2, ln2, TILES - 4, TILES, 1 + LN_EPS, LN_EPS * LN_EPS, var_step, 7, var_ready)
            ffn_step(1, 1)
            dve.wait_ge(r2_ready, 2)
            with dve.Fori(1, TILES // 2 - 1) as i:
                for p in range(2):
                    ffn_step(i * 2 + p, p)
            ffn_step(TILES - 2, 0, ahead=False)
            ffn_step(TILES - 1, 1, last=True, ahead=False)

        @block.tensor
        def _(pe):
            mm = nc.tensor.matmul
            pe.wait_ge(consts_pool, 4)

            def mm3(o, a, b, first=True, last=True):
                mm(o, a[1], b[0], start=first, stop=False)
                mm(o, a[0], b[1], start=False, stop=False)
                return mm(o, a[0], b[0], start=False, stop=last)

            def transpose_x(t, p):
                pe.wait_ge(xn_ready, t + 1)
                pe.wait_ge(ctx_loaded[p], (t - p) * 8 + 16)
                wait(pe, xT_ready, t)
                wait(pe, pT_ready, (t - 2) * 4)
                for k in range(KD):
                    nc.tensor.transpose(bank[7][:, k * P:(k + 1) * P], xn[:, p, k * P:(k + 1) * P], ident[:])
                nc.tensor.transpose(bank[7][:, 2 * P:3 * P], ctile[:, p, :], ident[:]).then_inc(xT_filled, 1)

            def project_qk(t):
                pe.wait_ge(xT_ready, t + 1)
                wait(pe, oT_ready, t - 2)
                for k in range(KD):
                    mm3(bank[4][:, 0:DIM], [h[:, k, :] for h in xT], [h[:, k, :] for h in wqkv],
                        first=(k == 0), last=(k == KD - 1))
                mm3(bank[4][:, DIM:2 * DIM], [h[:, KD, :] for h in xT], [h[:, KD, :] for h in wqkv])\
                    .then_inc(qk_filled, 1)

            def project_v(t):
                wait(pe, v_ready, t * 4)
                wait(pe, pT_ready, (t - 1) * 4)
                mm3(bank[6][:, 0:DIM], [h[:, KD, :] for h in xT], [h[:, KD + 1, :] for h in wqkv])\
                    .then_inc(v_filled, 1)

            def transpose_kq(t):
                pe.wait_ge(qk_roped, t * 2 + 2)
                wait(pe, sub_done, t * 4)
                nc.tensor.transpose(bank[2][:, 0:P], qkr[:, 1, 0:P], ident[:]).then_inc(kq_filled, 1)
                for k in range(KD):
                    nc.tensor.transpose(bank[3][:, k * P:(k + 1) * P], qkr[:, 0, k * P:(k + 1) * P], ident[:])
                nc.tensor.transpose(bank[3][:, DIM:DIM + P], qkr[:, 1, P:2 * P], ident[:]).then_inc(kq_filled, 1)

            def logits(t, g0, half):
                if half:
                    pe.wait_ge(k1_ready, t * 4 + 4)
                else:
                    pe.wait_ge(q_ready, t + 1)
                    pe.wait_ge(k0_ready, t + 1)
                for b in range(2):
                    for g in (g0, g0 + 1):
                        rows, cols = slice(32 * g, 32 * g + 32), slice(64 * b, 64 * b + 64)
                        m = mm(bank[g][cols, 256 * half:256 * half + 256].rearrange("p (j n) -> p j n", j=4),
                               qT[rows, half, cols], kT[rows, half, :, cols], start=True, stop=True)
                        if half and b:
                            m.then_inc(s_filled, 1)

            def transpose_p(t, p, gr, more=True):
                pe.wait_ge(p_ready, t * 4 + gr + 1)
                if gr == 0:
                    wait(pe, v_ready, t * 4 + 8 if more else TILES * 4)
                if gr == 1 and more:
                    pe.wait_ge(xT_ready, t + 3)
                if gr >= 2:
                    pe.wait_ge(pT_ready, t * 4 + gr - 1)
                for i in range(4):
                    m = nc.tensor.transpose(bank[6 + gr % 2][:, i * P:(i + 1) * P],
                                            pb[:, p, gr, 2 * i:2 * i + 2, :].rearrange("p h k -> p (h k)"),
                                            ident[:])
                m.then_inc(pT_filled, 1)

            def attend(t, p, roped=True):
                pe.wait_ge(pT_ready, t * 4 + 4)
                pe.wait_ge(v_ready, t * 4 + 4)
                if roped:
                    pe.wait_ge(ropeab_done, t * 2 + 6)
                else:
                    pe.wait_ge(oT_ready, t)
                def product(half, r, g, lhs, cols, c):
                    return mm(bank[4][32 * g:32 * g + 32, c:c + cols.stop - cols.start], lhs,
                              pT[:, 4 * g + 2 * half + r, cols], start=(r == 0), stop=(r == 1))

                for half in range(2):
                    for b in range(2):
                        for r in range(2):
                            for g in range(GROUPS):
                                c = 256 * r + 32 * (half * GROUPS + g)
                                product(half, r, g, vb[:, p, b].rearrange("p r c -> p (r c)")[:, c:c + 32],
                                        slice(64 * b, 64 * b + 64), half * P + b * 64)
                    for r in range(2):
                        for g in range(GROUPS):
                            m = product(half, r, g, hone[:, r, :], slice(0, P), DIM + half * P)
                m.then_inc(o_filled, 1)

            def project_out(t, k, b=5):
                if k == 0:
                    pe.wait_ge(oT_ready, t + 1)
                    wait(pe, x1_ready, t)
                m = mm(bank[b][:, 0:DIM], oT[:, k * P:(k + 1) * P], wo[:, k, :], start=(k == 0), stop=(k == KD - 1))
                if k == KD - 1:
                    m.then_inc(a_filled, 1)

            def mu_sums(s, q):
                pe.wait_ge(musq_ready, 3)
                pe.wait_ge(x1_ready, s - 2)
                for e in range(4 * q, 4 * q + 4):
                    m = mm(bank[5][:, DIM + e:DIM + e + 1], musq[0][:, e * SLOTS:(e + 1) * SLOTS], ones[:, 0:1],
                           start=True, stop=True)
                if q == 3:
                    m.then_inc(muss_ready, 1)

            def step(s, p, before=True, after=True, out=True, ahead=True, norms=None):
                if before:
                    transpose_p(s - 1, 1 - p, 0, more=after)
                logits(s, 0, 0)
                if before:
                    transpose_p(s - 1, 1 - p, 1, more=after)
                logits(s, 0, 1)
                if before:
                    transpose_p(s - 1, 1 - p, 2)
                if after and before:
                    project_qk(s + 1)
                logits(s, 2, 0)
                if norms is not None:
                    mu_sums(s, norms)
                if before:
                    transpose_p(s - 1, 1 - p, 3)
                logits(s, 2, 1)
                if norms == 3:
                    pe.wait_ge(muss_clamped, 1)
                if out:
                    for k in range(KD):
                        project_out(s - 2, k)
                if after:
                    project_v(s + 1)
                    if before:
                        attend(s - 1, 1 - p)
                    transpose_kq(s + 1)
                    if ahead:
                        transpose_x(s + 2, p)

            transpose_x(0, 0)
            pe.wait_ge(wqkv_ready, 1)
            project_qk(0)
            project_v(0)
            transpose_x(1, 1)
            transpose_kq(0)
            project_qk(1)
            step(0, 0, before=False, out=False)
            step(1, 1, out=False)
            pe.wait_ge(wo_loaded, 16)
            step(2, 0)
            for q in range(4):
                step(3 + q, (3 + q) % 2, norms=q)
            step(7, 1)
            pe.wait_ge(diag_ready, 1)
            pe.wait_ge(v_ready, 36)
            pe.wait_ge(xT_ready, 10)
            for c in range(4):
                if c == 2:
                    pe.wait_ge(x1_ready, 6)
                if c == 3:
                    pe.wait_ge(rb_ready, 1)
                mm(bank[NB[c]][:], ones[:], diag[:, 4 * c:4 * c + 4, :].rearrange("p e s -> p (e s)"),
                   start=True, stop=True).then_inc(rb_filled, 1)
            pe.wait_ge(rb_ready, 4)
            with pe.Fori(4, TILES // 2 - 1) as i:
                for p in range(2):
                    step(i * 2 + p, p)
            step(TILES - 2, 0, ahead=False)
            def transpose_xl(t, p):
                pe.wait_ge(xl_ready, t + 1)
                wait(pe, xw_ready, t * 4 - 2)
                for k in range(KD):
                    m = nc.tensor.transpose(bank[2][:, k * P:(k + 1) * P], xl[:, p, k * P:(k + 1) * P], ident[:])
                m.then_inc(xlT_filled, 1)

            def slot_logits(t):
                pe.wait_ge(xlT_ready, t + 1)
                for c in range(4):
                    if c < 2:
                        wait(pe, (eT_act, eT_dve)[c], (t * 2, t * 2 - 1)[c])
                    elif c == 3:
                        wait(pe, hn_ready, (t - 1) * len(HG) + 5)
                    for k in range(KD):
                        m = mm3(bank[LB[c]][:], [h[:, k, :] for h in xlT],
                                [h[:, k, c * BANK:(c + 1) * BANK] for h in mun], first=(k == 0), last=(k == KD - 1))
                    m.then_inc(l_filled, 1)

            def expand(t):
                pe.wait_ge(e_ready, t * 4 + 3)
                for c in range(2):
                    for k in range(KD):
                        m = mm3(bank[2 + c][:], [h[:, k, :] for h in xlT],
                                [h[:, k, c * BANK:(c + 1) * BANK] for h in w1], first=(k == 0), last=(k == KD - 1))
                    m.then_inc(xw_filled, 1)

            def transpose_e(t):
                for gr in range(4):
                    pe.wait_ge(e_ready, t * 4 + gr + 1)
                    for i in range(4):
                        m = nc.tensor.transpose(bank[(6, 7, 0, 1)[gr]][:, i * P:(i + 1) * P], eb[:, 4 * gr + i, :],
                                                ident[:])
                    m.then_inc(eT_filled, 1)

            def dispatch(t):
                pe.wait_ge(xw_ready, t * 4 + 4)
                for i, gr in enumerate(HG):
                    if i == 0:
                        wait(pe, yo_ready, t)
                    if i >= 3:
                        pe.wait_ge(hn_ready, t * len(HG) + i - 2)
                    for n, e in enumerate(gr):
                        m = mm(bank[HB[i % 3]][:, n * 2 * HC:(n + 1) * 2 * HC], eb[:, e, :], xw[:, e, :],
                               start=True, stop=True)
                    m.then_inc(h_filled, 1)

            def combine(t, last):
                pe.wait_ge(es_ready, t + 1)
                pe.wait_ge(eT_act, t * 2 + (4 if last else 2))
                pe.wait_ge(eT_dve, t * 2 + (0 if last else 2))
                nc.tensor.transpose(bank[7][0:EXPERTS, 0:P], es[:], ident[:]).then_inc(esT_filled, 1)
                for c in range(2):
                    pe.wait_ge(h_ready, t * len(GG) + c + 2)
                    for i in range(4):
                        for b in range(2):
                            for r in range(2):
                                e = 8 * c + 2 * i + r
                                m = mm((bank[6], bank[3])[c][64 * r:64 * r + 64, i * P + b * 64:i * P + b * 64 + 64],
                                       hb[:, e, b, :], eT[:, e, b * 64:b * 64 + 64], start=True, stop=True)
                    m.then_inc(g_filled, 1)

            def contract(t):
                pe.wait_ge(esT_ready, t + 1)
                mm(bank[4][:, 0:DIM], esT[:], b2s[:], start=True, stop=False)
                for i in range(EXPERTS // 2):
                    pe.wait_ge(gT_ready, t * 2 + i // 4 + 1)
                    m = mm3(bank[4][:, 0:DIM], [h[:, i, :] for h in gT], [h[:, i, :] for h in w2],
                            first=False, last=(i == EXPERTS // 2 - 1))
                m.then_inc(y_filled, 1)

            def ffn_step(s, p, last=False, expanded=False):
                if not expanded:
                    expand(s)
                transpose_e(s)
                if expanded:
                    pe.wait_ge(x1_ready, TILES)
                if not last:
                    transpose_xl(s + 1, 1 - p)
                dispatch(s)
                if not last:
                    slot_logits(s + 1)
                combine(s, last)
                contract(s)

            step(TILES - 1, 1, after=False, ahead=False)
            attend(TILES - 2, 0, roped=False)
            pe.wait_ge(sub_done, TILES * 4)
            transpose_xl(0, 0)
            for gr in range(2):
                transpose_p(TILES - 1, 1, gr, more=False)
            pe.wait_ge(x1_ready, TILES - 2)
            pe.wait_ge(mu_ready, 2)
            slot_logits(0)
            for gr in range(2, 4):
                transpose_p(TILES - 1, 1, gr, more=False)
            for k in range(KD):
                project_out(TILES - 2, k, 3)
            attend(TILES - 1, 1, roped=False)
            pe.wait_ge(x1_ready, TILES - 1)
            pe.wait_ge(w12_ready, 2)
            expand(0)
            pe.wait_ge(wb_loaded, 64)
            pe.wait_ge(e_ready, 4)
            for k in range(KD):
                project_out(TILES - 1, k)
            ffn_step(0, 0, expanded=True)
            ffn_step(1, 1)
            with pe.Fori(1, TILES // 2 - 1) as i:
                for p in range(2):
                    ffn_step(i * 2 + p, p)
            ffn_step(TILES - 2, 0)
            ffn_step(TILES - 1, 1, last=True)


_INS = ['x', 'ctx_1024', 'fside_BxSx2_0', 'L0_xattn_Wq', 'L0_xattn_Wkv', 'L0_xattn_Wout', 'L0_xattn_bout',
        'L0_ffn_gamma', 'L0_ffn_beta', 'L0_ffn_mu', 'L0_ffn_scale', 'L0_ffn_W1', 'L0_ffn_b1', 'L0_ffn_W2',
        'L0_ffn_b2']


def kernel(**inputs):
    import numpy as _np
    import concourse.bacc as _bacc
    from concourse import mybir as _mybir
    from concourse.bass_utils import run_bass_kernel_spmd as _run

    nc = _bacc.Bacc("TRN2", target_bir_lowering=False, num_devices=1)
    arrays, args = {}, []
    for name in _INS:
        a = _np.ascontiguousarray(inputs[name])
        arrays[f"in_{name}"] = a
        args.append(nc.dram_tensor(f"in_{name}", a.shape, _mybir.dt.from_np(a.dtype), kind="ExternalInput").ap())
    out = nc.dram_tensor("out", (BATCH, SEQ, DIM), F32, kind="ExternalOutput").ap()
    build(nc, *args, out)
    r = _run(nc, [arrays], core_ids=[0])
    return r.results[0]["out"]
```
